# Optimizing a Trainium2 kernel written in Bass

```python
import numpy as np
import jax
import jax.numpy as jnp

def _softmax(x, axis=-1):
    return jax.nn.softmax(x, axis=axis)

def _gelu(x):
    return jax.nn.gelu(x, approximate=True)

def _silu(x):
    return jax.nn.silu(x)

def _sigmoid(x):
    return jax.nn.sigmoid(x)

def _layernorm(x, axis=-1, eps=1e-05):
    m = jnp.mean(x, axis=axis, keepdims=True)
    v = jnp.var(x, axis=axis, keepdims=True)
    return (x - m) / jnp.sqrt(v + eps)

def _scatter_add(tgt, idx, src, axis=0):
    return tgt.at[idx].add(src)

def _segment_sum(src, seg, n):
    return jax.ops.segment_sum(src, seg, n)
kernel_name = 'mk_adj_resnorm_d2_adj_r2_fcbe18'

def setup_inputs(seed: int=0):
    np.random.seed(seed)
    _w = jnp.asarray

    def _rec_inputs():
        import jax
        import jax.numpy as jnp
        _gk = jax.random.key(seed)
        x = -0.0003929 + 0.9999 * jax.random.normal(jax.random.fold_in(_gk, 1), (8, 1024, 256), jnp.float32)
        _w = (1.0 + jnp.arange(1024, dtype=jnp.float32)) ** (-0.5)
        _w = _w / _w.mean()
        _pij = jnp.clip(0.0078125 * _w[:, None] * _w[None, :], 0.0, 1.0)
        _a = jax.random.uniform(jax.random.fold_in(_gk, 2), (1024, 1024)) < _pij
        _a = jnp.logical_or(_a, jnp.eye(1024, dtype=bool))
        _af = _a.astype(jnp.float32)
        _af = _af * jax.random.uniform(jax.random.fold_in(_gk, 3), (1024, 1024), jnp.float32, 0.05, 1)
        adj = _af
        return (x, adj)
    x, adj = _rec_inputs()

    def _L0_gnn_setup():
        import jax, jax.numpy as jnp
        import numpy as np
        B, N, D, O = (8, 2048, 256, 256)
        key = jax.random.key(seed)
        k1, k2, k3, k4 = jax.random.split(key, 4)
        x = jax.random.normal(k1, (B, N, D), dtype=jnp.float32)
        adj = jax.random.uniform(k2, (N, N), dtype=jnp.float32)
        weight = jax.random.normal(k3, (D, O), dtype=jnp.float32) * 0.02
        bias = jax.random.normal(k4, (O,), dtype=jnp.float32) * 0.02
        return {'x': x, 'adj': adj, 'weight': weight, 'bias': bias}
    _L0_gnn_all = _L0_gnn_setup()
    _L0_gnn_in = {k: v for k, v in _L0_gnn_all.items() if k in ('weight', 'bias')}
    del _L0_gnn_all

    def _L1_gnn_setup():
        import jax, jax.numpy as jnp
        import numpy as np
        B, N, D, H = (4, 1024, 256, 8)
        HD = D // H
        key = jax.random.key(seed)
        ks = jax.random.split(key, 10)
        x = jax.random.normal(ks[0], (B, N, D), dtype=jnp.float32)
        adj = (jax.random.uniform(ks[1], (N, N)) < 0.1).astype(jnp.float32)
        s = 1.0 / np.sqrt(D)
        Wq = jax.random.normal(ks[2], (D, D), dtype=jnp.float32) * s
        Wk = jax.random.normal(ks[3], (D, D), dtype=jnp.float32) * s
        Wv = jax.random.normal(ks[4], (D, D), dtype=jnp.float32) * s
        Wo = jax.random.normal(ks[5], (D, D), dtype=jnp.float32) * s
        bq = jnp.zeros((D,), jnp.float32)
        bk = jnp.zeros((D,), jnp.float32)
        bv = jnp.zeros((D,), jnp.float32)
        bo = jnp.zeros((D,), jnp.float32)
        return {'x': x, 'adj': adj, 'Wq': Wq, 'bq': bq, 'Wk': Wk, 'bk': bk, 'Wv': Wv, 'bv': bv, 'Wo': Wo, 'bo': bo}
    _L1_gnn_all = _L1_gnn_setup()
    _L1_gnn_in = {k: v for k, v in _L1_gnn_all.items() if k in ('Wq', 'bq', 'Wk', 'bk', 'Wv', 'bv', 'Wo', 'bo')}
    del _L1_gnn_all
    return {'x': x, 'adj': adj, 'L0_gnn_weight': _L0_gnn_in['weight'], 'L0_gnn_bias': _L0_gnn_in['bias'], 'L1_gnn_Wq': _L1_gnn_in['Wq'], 'L1_gnn_bq': _L1_gnn_in['bq'], 'L1_gnn_Wk': _L1_gnn_in['Wk'], 'L1_gnn_bk': _L1_gnn_in['bk'], 'L1_gnn_Wv': _L1_gnn_in['Wv'], 'L1_gnn_bv': _L1_gnn_in['bv'], 'L1_gnn_Wo': _L1_gnn_in['Wo'], 'L1_gnn_bo': _L1_gnn_in['bo']}

def reference(x, adj, L0_gnn_weight, L0_gnn_bias, L1_gnn_Wq, L1_gnn_bq, L1_gnn_Wk, L1_gnn_bk, L1_gnn_Wv, L1_gnn_bv, L1_gnn_Wo, L1_gnn_bo):
    import jax
    import jax.numpy as jnp

    def _L0_gnn_ref(x, adj, weight, bias):
        import jax, jax.numpy as jnp
        import numpy as np
        B, N, D, O = (8, 2048, 256, 256)
        y = jnp.einsum('nm,bmd->bnd', adj, x)
        out = jnp.einsum('bnd,do->bno', y, weight) + bias
        return out

    def _L1_gnn_ref(x, adj, Wq, bq, Wk, bk, Wv, bv, Wo, bo):
        import jax, jax.numpy as jnp
        import numpy as np
        B, N, D, H = (4, 1024, 256, 8)
        HD = D // H
        b, n, d = x.shape
        q = (x @ Wq + bq).reshape(b, n, H, HD)
        k = (x @ Wk + bk).reshape(b, n, H, HD)
        v = (x @ Wv + bv).reshape(b, n, H, HD)
        scores = jnp.einsum('bqhd,bkhd->bhqk', q, k) / jnp.sqrt(jnp.float32(HD))
        scores = scores + (1.0 - adj)[None, None, :, :] * -1000000000.0
        attn = jax.nn.softmax(scores, axis=-1)
        out = jnp.einsum('bhqk,bkhd->bqhd', attn, v).reshape(b, n, d)
        return out @ Wo + bo
    x = _layernorm(x + _L0_gnn_ref(x, adj, L0_gnn_weight, L0_gnn_bias), axis=-1)
    x = _layernorm(x + _L1_gnn_ref(x, adj, L1_gnn_Wq, L1_gnn_bq, L1_gnn_Wk, L1_gnn_bk, L1_gnn_Wv, L1_gnn_bv, L1_gnn_Wo, L1_gnn_bo), axis=-1)
    return x

_drawn_inputs = setup_inputs


def setup_inputs(seed=0):
    import zlib

    import numpy as np

    out = dict(_drawn_inputs(seed))
    spreads = {'L1_gnn_bq': (0.0, 0.1),
     'L1_gnn_bk': (0.0, 0.1),
     'L1_gnn_bv': (0.0, 0.1),
     'L1_gnn_bo': (0.0, 0.1)}
    factors = {'L0_gnn_bias': 3.359}
    for name, (base, spread) in spreads.items():
        noise = np.random.default_rng([zlib.crc32(name.encode()), seed]).standard_normal(out[name].shape)
        drawn = base * np.exp(spread * noise) if base else spread * noise
        out[name] = jnp.asarray(drawn.astype(out[name].dtype))
    for name, factor in factors.items():
        out[name] = (out[name] * factor).astype(out[name].dtype)
    return out
```

```python
from contextlib import ExitStack

import concourse.bass as bass
from concourse import mybir

F32 = mybir.dt.float32
F32R = mybir.dt.float32r
ALU = mybir.AluOpType
ACT = mybir.ActivationFunctionType

P = 128
BANK = 512
HEADS = 8
EPS = 1e-5
MASKED = 1.0e9
FAR = 3.0e38
W0, WQ, WK, WV, WO = range(5)


def split_terms(hi_a, lo_a, hi_b, lo_b):
    return ((hi_a, hi_b), (lo_a, hi_b), (hi_a, lo_b))


def build(nc, x, adj, weights, biases, out):
    B, N, D = x.shape
    NT = N // P
    DC = D // P
    HALVES = N // BANK
    TPH = BANK // P
    HD = D // HEADS
    HG = P // HD
    GROUPS = HEADS // HG
    SCALE = float(HD) ** -0.5
    x1_dram = nc.dram_tensor("x1_rows", (B, N, D), F32, kind="Internal").ap()

    with ExitStack() as whole:
        def sb(ctx, name, shape, dt=F32):
            return ctx.enter_context(nc.sbuf_tensor(name, shape, dt))

        def sem(ctx, name):
            return ctx.enter_context(nc.semaphore(name))

        psum = whole.enter_context(nc.psum_tensor("psum", [P, 8, BANK], F32))
        ident = sb(whole, "ident", [P, P])
        mask = sb(whole, "mask", [P, NT, N])
        w_hi = sb(whole, "w_hi", [P, 5, DC, D], F32R)
        w_lo = sb(whole, "w_lo", [P, 5, DC, D], F32R)
        b_rows = sb(whole, "b_rows", [P, 3, D])
        b_cols = sb(whole, "b_cols", [P, 2, GROUPS])
        b_in = sb(whole, "b_in", [P, 2, GROUPS])
        eps = sb(whole, "eps", [P, 1])
        mask_ready = sem(whole, "mask_ready")

        layer_norm_1(nc, sb, sem, x, adj, weights, biases, x1_dram, psum, ident, mask, w_hi, w_lo,
                     b_rows, b_cols, b_in, eps, mask_ready, (B, N, D, NT, DC, HALVES, TPH, GROUPS, SCALE))
        layer_norm_2(nc, sb, sem, x1_dram, out, psum, ident, mask, w_hi, w_lo, b_rows, b_cols, eps,
                     mask_ready, (B, N, D, NT, DC, HALVES, TPH, HD, HG, GROUPS))


def layer_norm_1(nc, sb, sem, x, adj, weights, biases, x1_dram, psum, ident, mask, w_hi, w_lo,
                 b_rows, b_cols, b_in, eps, mask_ready, sizes):
    B, N, D, NT, DC, HALVES, TPH, GROUPS, SCALE = sizes
    CH = HALVES * DC
    HB = NT // 2
    PAIRS = B // 2
    with ExitStack() as ctx:
        adjT_hi = sb(ctx, "adjT_hi", [P, NT, N], F32R)
        adjT_lo = sb(ctx, "adjT_lo", [P, NT, N], F32R)
        xin = sb(ctx, "xin", [P, 2, NT, D])
        x_hi = sb(ctx, "x_hi", [P, 2, NT, D], F32R)
        x_lo = sb(ctx, "x_lo", [P, 2, NT, D], F32R)
        yT_hi = sb(ctx, "yT_hi", [P, DC, N], F32R)
        yT_lo = sb(ctx, "yT_lo", [P, DC, N], F32R)
        w_in = sb(ctx, "w_in", [P, 5, DC, D])
        stats = sb(ctx, "stats", [P, NT, 6])
        moments = sb(ctx, "moments", [P, NT, 2])
        std = sb(ctx, "std", [P, NT])
        rstd = sb(ctx, "rstd", [P, NT])

        adj_loaded = [sem(ctx, f"adj_loaded{h}") for h in range(HALVES)]
        w_loaded = sem(ctx, "w_loaded")
        b_loaded = sem(ctx, "b_loaded")
        x_loaded = [sem(ctx, f"x_loaded{u}") for u in range(2)]
        x1_stored = [sem(ctx, f"x1_stored{u}") for u in range(2)]
        zeroed = sem(ctx, "zeroed")
        ident_ready = sem(ctx, "ident_ready")
        eps_ready = sem(ctx, "eps_ready")
        wq_scaled = sem(ctx, "wq_scaled")
        w_hi_ready = sem(ctx, "w_hi_ready")
        w_lo_ready = sem(ctx, "w_lo_ready")
        adj_turned = sem(ctx, "adj_turned")
        adjT_hi_ready = sem(ctx, "adjT_hi_ready")
        adjT_lo_ready = sem(ctx, "adjT_lo_ready")
        x_hi_ready = sem(ctx, "x_hi_ready")
        x_lo_ready = sem(ctx, "x_lo_ready")
        xb_ready = sem(ctx, "xb_ready")
        yT_done = sem(ctx, "yT_done")
        yT_hi_ready = sem(ctx, "yT_hi_ready")
        yT_lo_ready = sem(ctx, "yT_lo_ready")
        h_done = sem(ctx, "h_done")
        h_ready = sem(ctx, "h_ready")
        stats_ready = sem(ctx, "stats_ready")
        moments_ready = sem(ctx, "moments_ready")
        std_ready = sem(ctx, "std_ready")
        rstd_ready = sem(ctx, "rstd_ready")
        x1_ready = sem(ctx, "x1_ready")
        passed = sem(ctx, "passed")

        def rows(dram, b):
            return dram[b].rearrange("(t p) d -> p t d", p=P)

        block = ctx.enter_context(nc.Block())

        @block.sync
        def _(sp):
            adj_rows = adj.rearrange("(t p) m -> p t m", p=P)
            for h in range(HALVES):
                sp.dma_start(mask[:, h * TPH:(h + 1) * TPH, :], adj_rows[:, h * TPH:(h + 1) * TPH, :]) \
                  .then_inc(adj_loaded[h], 16)
                sp.dma_start(xin[:, h], rows(x, h)).then_inc(x_loaded[h], 16)
            for i, w in enumerate(weights):
                sp.dma_start(w_in[:, i], w.rearrange("(c p) n -> p c n", p=P)).then_inc(w_loaded, 16)
            for i, v in enumerate((biases[0], biases[3], biases[4])):
                sp.dma_start(b_rows[:, i, :], v.rearrange("(a d) -> a d", a=1).broadcast_to([P, D])) \
                  .then_inc(b_loaded, 16)
            with nc.allow_non_contiguous_dma(reason="one feature per partition"):
                for i in range(2):
                    sp.dma_start(b_in[:, i, :], biases[1 + i].rearrange("(g p) -> p g", p=P)) \
                      .then_inc(b_loaded, 16)

            def store(b, j, u):
                sp.wait_ge(x1_ready, b + 1)
                sp.dma_start(rows(x1_dram, b), xin[:, u]).then_inc(x1_stored[u], 16)

            with sp.Fori(0, PAIRS - 1) as j:
                for u in range(2):
                    store(2 * j + u, j, u)
                    sp.wait_ge(x1_stored[u], 16 * j + 16)
                    sp.dma_start(xin[:, u], rows(x, 2 * j + u + 2)).then_inc(x_loaded[u], 16)
            for u in range(2):
                store(B - 2 + u, PAIRS - 1, u)
            for u in range(2):
                sp.wait_ge(x1_stored[u], 16 * PAIRS)

        @block.gpsimd
        def _(pool):
            pool.memset(ident[:], 0.0).then_inc(zeroed, 1)
            pool.wait_ge(zeroed, 1)
            pool.affine_select(out=ident[:], in_=ident[:], compare_op=ALU.not_equal, fill=1.0, base=0,
                               pattern=[[-1, P]], channel_multiplier=1).then_inc(ident_ready, 1)
            pool.memset(eps[:], EPS).then_inc(eps_ready, 1)

            def x_parts(b, j, u):
                pool.wait_ge(x_hi_ready, b + 1)
                pool.tensor_tensor(x_lo[:, u], xin[:, u], x_hi[:, u].bitcast(F32), ALU.subtract) \
                    .then_inc(x_lo_ready, 1)
                pool.tensor_tensor(xin[:, u], xin[:, u],
                                   b_rows[:, 0:1, :].broadcast_to([P, NT, D]), ALU.add).then_inc(xb_ready, 1)

            pool.wait_ge(w_hi_ready, 1)
            pool.wait_ge(wq_scaled, 2)
            pool.tensor_tensor(w_lo[:], w_in[:], w_hi[:].bitcast(F32), ALU.subtract).then_inc(w_lo_ready, 1)
            pool.wait_ge(b_loaded, 16 * 5)
            with pool.Fori(0, PAIRS) as j:
                for u in range(2):
                    x_parts(2 * j + u, j, u)

        @block.scalar
        def _(act):
            def x_high(b, j, u):
                act.wait_ge(x_loaded[u], 16 * j + 16)
                act.activation(x_hi[:, u], xin[:, u], ACT.Copy).then_inc(x_hi_ready, 1)

            x_high(0, 0, 0)
            act.wait_ge(wq_scaled, 2)
            act.activation(w_hi[:], w_in[:], ACT.Copy).then_inc(w_hi_ready, 1)
            for f in range(HALVES * NT):
                act.wait_ge(adj_turned, f + 1)
                act.activation(adjT_hi[:, f % NT, (f // NT) * BANK:(f // NT + 1) * BANK], psum[:, f % 8, :],
                               ACT.Copy).then_inc(adjT_hi_ready, 1)

            def batch(b, j, u, last):
                for c in range(CH):
                    h, dc = divmod(c, DC)
                    act.wait_ge(yT_done, CH * b + c + 1)
                    act.activation(yT_hi[:, dc, h * BANK:(h + 1) * BANK], psum[:, c, :],
                                   ACT.Copy).then_inc(yT_hi_ready, 1)
                    if c == CH - 2 and not last:
                        x_high(b + 1, j + u, 1 - u)
                act.wait_ge(moments_ready, b + 1)
                act.activation(std[:], moments[:, :, 1], ACT.Sqrt, bias=eps[:, 0:1]).then_inc(std_ready, 1)

            act.wait_ge(eps_ready, 1)
            with act.Fori(0, PAIRS - 1) as j:
                for u in range(2):
                    batch(2 * j + u, j, u, False)
            for u in range(2):
                batch(B - 2 + u, PAIRS - 1, u, u == 1)

        @block.vector
        def _(dve):
            dve.wait_ge(w_loaded, 16 * 5)
            dve.tensor_scalar(w_in[:, WQ], w_in[:, WQ], -SCALE, None, ALU.mult).then_inc(wq_scaled, 1)
            dve.wait_ge(b_loaded, 16 * 5)
            dve.tensor_scalar(b_cols[:, 0, :], b_in[:, 0, :], -SCALE, None, ALU.mult).then_inc(wq_scaled, 1)
            dve.tensor_copy(b_cols[:, 1, :], b_in[:, 1, :]).then_inc(wq_scaled, 1)
            for f in range(HALVES * NT):
                dve.wait_ge(adjT_hi_ready, f + 1)
                cols = slice((f // NT) * BANK, (f // NT + 1) * BANK)
                dve.tensor_tensor(adjT_lo[:, f % NT, cols], psum[:, f % 8, :],
                                  adjT_hi[:, f % NT, cols].bitcast(F32), ALU.subtract).then_inc(adjT_lo_ready, 1)
            dve.wait_ge(adj_turned, HALVES * NT)
            dve.tensor_scalar(mask[:], mask[:], 1.0, -MASKED, ALU.subtract, ALU.mult).then_inc(mask_ready, 1)

            def batch(b, j, u):
                for c in range(CH):
                    h, dc = divmod(c, DC)
                    cols = slice(h * BANK, (h + 1) * BANK)
                    dve.wait_ge(yT_hi_ready, CH * b + c + 1)
                    dve.tensor_tensor(yT_lo[:, dc, cols], psum[:, c, :], yT_hi[:, dc, cols].bitcast(F32),
                                      ALU.subtract).then_inc(yT_lo_ready, 1)
                dve.wait_ge(xb_ready, b + 1)
                for w in range(HB):
                    h2 = xin[:, u, 2 * w:2 * w + 2, :]
                    dve.wait_ge(h_done, HB * b + w + 1)
                    dve.tensor_tensor(h2, psum[:, 4 + w, :].rearrange("p (t d) -> p t d", t=2), h2, ALU.add) \
                       .then_inc(h_ready, 1)
                for t in range(NT):
                    dve.wait_ge(h_ready, HB * b + t // 2 + 1)
                    dve.bn_stats(stats[:, t, :], xin[:, u, t, :]).then_inc(stats_ready, 1)
                dve.wait_ge(stats_ready, NT * b + NT)
                dve.sem_inc(passed, 1)
                for t in range(NT):
                    ins = dve.bn_aggr(moments[:, t, :], stats[:, t, :])
                ins.then_inc(moments_ready, 1)
                dve.wait_ge(std_ready, b + 1)
                dve.reciprocal(rstd[:], std[:]).then_inc(rstd_ready, 1)
                dve.wait_ge(rstd_ready, b + 1)
                for t in range(NT):
                    ins = dve.tensor_scalar(xin[:, u, t, :], xin[:, u, t, :], moments[:, t, 0:1],
                                            rstd[:, t:t + 1], ALU.subtract, ALU.mult)
                ins.then_inc(x1_ready, 1)

            with dve.Fori(0, PAIRS) as j:
                for u in range(2):
                    batch(2 * j + u, j, u)

        @block.tensor
        def _(pe):
            pe.wait_ge(ident_ready, 1)
            for h in range(HALVES):
                pe.wait_ge(adj_loaded[h], 16)
                for mt in range(NT):
                    f = h * NT + mt
                    if f >= 8:
                        pe.wait_ge(adjT_lo_ready, f - 7)
                    for t in range(TPH):
                        ins = pe.transpose(psum[:, f % 8, t * P:(t + 1) * P],
                                           mask[:, h * TPH + t, mt * P:(mt + 1) * P], ident[:])
                    ins.then_inc(adj_turned, 1)
            pe.wait_ge(adjT_lo_ready, HALVES * NT)
            pe.wait_ge(w_lo_ready, 1)

            def chunk(b, u, c):
                h, dc = divmod(c, DC)
                for mt in range(NT):
                    cols = slice(h * BANK, (h + 1) * BANK)
                    terms = split_terms(x_hi[:, u, mt, dc * P:(dc + 1) * P], x_lo[:, u, mt, dc * P:(dc + 1) * P],
                                        adjT_hi[:, mt, cols], adjT_lo[:, mt, cols])
                    for n, (lhsT, rhs) in enumerate(terms):
                        ins = pe.matmul(psum[:, c, :], lhsT, rhs, start=(mt == 0 and n == 0),
                                        stop=(mt == NT - 1 and n == 2))
                ins.then_inc(yT_done, 1)

            def project(b, w):
                for t in range(2):
                    cols = slice((2 * w + t) * P, (2 * w + t + 1) * P)
                    for dc in range(DC):
                        terms = split_terms(yT_hi[:, dc, cols], yT_lo[:, dc, cols], w_hi[:, W0, dc], w_lo[:, W0, dc])
                        for n, (lhsT, rhs) in enumerate(terms):
                            ins = pe.matmul(psum[:, 4 + w, t * D:(t + 1) * D], lhsT, rhs,
                                            start=(dc == 0 and n == 0), stop=(dc == DC - 1 and n == 2))
                ins.then_inc(h_done, 1)

            def batch(b, j, u):
                pe.wait_ge(x_lo_ready, b + 1)
                for c in range(CH - 1):
                    chunk(b, u, c)
                pe.wait_ge(yT_lo_ready, CH * b + DC)
                for w in range(HB // 2):
                    project(b, w)
                chunk(b, u, CH - 1)
                pe.wait_ge(yT_lo_ready, CH * b + CH)
                for w in range(HB // 2, HB):
                    project(b, w)

            with pe.Fori(0, PAIRS) as j:
                for u in range(2):
                    batch(2 * j + u, j, u)


def layer_norm_2(nc, sb, sem, x1_dram, out, psum, ident, mask, w_hi, w_lo, b_rows, b_cols, eps,
                 mask_ready, sizes):
    B, N, D, NT, DC, HALVES, TPH, HD, HG, GROUPS = sizes
    XF = DC * HALVES
    QF = GROUPS * 2 * HALVES
    VF = NT // 2
    STEPS = HEADS * NT
    SETS = GROUPS * NT
    T_LAG = 2
    R_LAG = HG - 1 + T_LAG
    AV_STEPS = HG - 1
    O_LAG = R_LAG + 1 + AV_STEPS
    T_BANK, T_RING = 4, 3
    O_BANK = 7
    with ExitStack() as ctx:
        x1 = sb(ctx, "x1", [P, NT, D])
        h = sb(ctx, "h", [P, NT, D])
        fT_hi = sb(ctx, "fT_hi", [P, DC, N], F32R)
        fT_lo = sb(ctx, "fT_lo", [P, DC, N], F32R)
        q_parts = sb(ctx, "q_parts", [P, HEADS, N], F32R)
        k_parts = sb(ctx, "k_parts", [P, HEADS, N], F32R)
        v = sb(ctx, "v", [P, NT, D])
        probs = sb(ctx, "probs", [P, 2, N])
        probsT = sb(ctx, "probsT", [P, 2, HG * N])
        far = sb(ctx, "far", [P, STEPS])
        sums = sb(ctx, "sums", [P, SETS, HG])
        recip = sb(ctx, "recip", [P, SETS, HG])
        ones = sb(ctx, "ones", [P, HD])
        recip_wide = sb(ctx, "recip_wide", [P, 2, HG, HD])
        recipT = sb(ctx, "recipT", [P, 2, P])
        o_full = sb(ctx, "o_full", [P, 2, P])
        stats = sb(ctx, "stats2", [P, NT, 6])
        moments = sb(ctx, "moments2", [P, NT, 2])
        std = sb(ctx, "std2", [P, NT])
        rstd = sb(ctx, "rstd2", [P, NT])

        x1_loaded = sem(ctx, "x1_loaded")
        res_loaded = sem(ctx, "res_loaded")
        stored = sem(ctx, "stored")
        ones_ready = sem(ctx, "ones_ready")
        res_ready = sem(ctx, "res_ready")
        x1_turned = sem(ctx, "x1_turned")
        x1T_hi_ready = sem(ctx, "x1T_hi_ready")
        x1T_lo_ready = sem(ctx, "x1T_lo_ready")
        qk_done = sem(ctx, "qk_done")
        qk_hi_ready = sem(ctx, "qk_hi_ready")
        qk_lo_ready = sem(ctx, "qk_lo_ready")
        parts_placed = [sem(ctx, f"parts_placed{i}") for i in range(HEADS)]
        v_done = sem(ctx, "v_done")
        v_ready = sem(ctx, "v_ready")
        scores_done = sem(ctx, "scores_done")
        masked = sem(ctx, "masked")
        probs_ready = sem(ctx, "probs_ready")
        turned = sem(ctx, "turned")
        even_taken = sem(ctx, "even_taken")
        odd_taken = sem(ctx, "odd_taken")
        recip_ready = sem(ctx, "recip_ready")
        wide_ready = sem(ctx, "wide_ready")
        recip_turned = sem(ctx, "recip_turned")
        recipT_ready = sem(ctx, "recipT_ready")
        av_done = sem(ctx, "av_done")
        o_ready = sem(ctx, "o_ready")
        o_lo_ready = sem(ctx, "o_lo_ready")
        proj_done = sem(ctx, "proj_done")
        h_ready = sem(ctx, "h_ready2")
        stats_ready = sem(ctx, "stats_ready2")
        moments_ready = sem(ctx, "moments_ready2")
        std_ready = sem(ctx, "std_ready2")
        rstd_ready = sem(ctx, "rstd_ready2")
        normed = sem(ctx, "normed")
        passed = sem(ctx, "passed2")

        def rows(dram, b):
            return dram[b].rearrange("(t p) d -> p t d", p=P)

        def staged(g):
            return probsT[:, g, :].rearrange("p (w n) -> p w n", w=HG)

        def probsT_of(g):
            return probsT[:, g % 2, :].rearrange("p (h k q) -> p h k q", h=HG, k=NT)

        def slot(i):
            return psum[:, 2 * (i % 2):2 * (i % 2) + 2, :].rearrange("p a n -> p (a n)")

        def at(b, per, n):
            assert n > 0
            return b * per + n

        block = ctx.enter_context(nc.Block())

        @block.sync
        def _(sp):
            def place(b, g):
                sp.wait_ge(qk_lo_ready, at(b, QF, QF // GROUPS * (g + 1)))
                for hh in range(HG):
                    head = HG * g + hh
                    own = slice(hh * HD, (hh + 1) * HD)
                    for r in range(4):
                        to = slice(r * HD, (r + 1) * HD)
                        sp.dma_start(q_parts[to, head, :].bitcast(F32), staged(g)[own, r % 2, :]) \
                          .then_inc(parts_placed[head], 16)
                        sp.dma_start(k_parts[to, head, :].bitcast(F32), staged(g)[own, 2 + r // 2, :]) \
                          .then_inc(parts_placed[head], 16)

            def residual(b):
                sp.dma_start(h[:], rows(x1_dram, b)).then_inc(res_loaded, 16)

            def middle(b):
                for g in range(GROUPS):
                    place(b, g)

            def result(b):
                sp.wait_ge(normed, b + 1)
                sp.dma_start(rows(out, b), h[:]).then_inc(stored, 16)

            sp.dma_start(x1[:], rows(x1_dram, 0)).then_inc(x1_loaded, 16)
            residual(0)
            with sp.Fori(0, B - 1) as b:
                middle(b)
                sp.wait_ge(x1_turned, at(b, XF, XF))
                sp.dma_start(x1[:], rows(x1_dram, b + 1)).then_inc(x1_loaded, 16)
                result(b)
                sp.wait_ge(stored, 16 * b + 16)
                residual(b + 1)
            middle(B - 1)
            result(B - 1)
            sp.wait_ge(stored, 16 * B)

        @block.gpsimd
        def _(pool):
            pool.memset(ones[:], 1.0).then_inc(ones_ready, 1)
            pool.wait_ge(ones_ready, 1)
            with pool.Fori(0, B) as b:
                pool.wait_ge(res_loaded, 16 * b + 16)
                pool.tensor_tensor(h[:], h[:], b_rows[:, 2:3, :].broadcast_to([P, NT, D]), ALU.add) \
                    .then_inc(res_ready, 1)

                def widen(s):
                    pool.wait_ge(recip_ready, at(b, SETS, s + 1))
                    if s >= 2:
                        pool.wait_ge(recip_turned, at(b, SETS, s - 1))
                    pool.tensor_tensor(recip_wide[:, s % 2], recip[:, s, :].rearrange("p (h a) -> p h a", a=1)
                                       .broadcast_to([P, HG, HD]),
                                       ones[:].rearrange("p (a d) -> p a d", a=1).broadcast_to([P, HG, HD]),
                                       ALU.mult).then_inc(wide_ready, 1)

                def o_low(s):
                    cols = slice((s % NT) * P, (s % NT + 1) * P)
                    pool.wait_ge(o_ready, at(b, SETS, s + 1))
                    pool.tensor_tensor(fT_lo[:, s // NT, cols], o_full[:, s % 2],
                                       fT_hi[:, s // NT, cols].bitcast(F32), ALU.subtract) \
                        .then_inc(o_lo_ready, 1)

                for s in range(SETS + 1):
                    if s < SETS:
                        widen(s)
                    if s >= 1:
                        o_low(s - 1)

        @block.scalar
        def _(act):
            with act.Fori(0, B) as b:
                for f in range(XF):
                    act.wait_ge(x1_turned, at(b, XF, f + 1))
                    act.activation(fT_hi[:, f // HALVES, (f % HALVES) * BANK:(f % HALVES + 1) * BANK],
                                   psum[:, 4 + f % 4, :], ACT.Copy).then_inc(x1T_hi_ready, 1)
                for f in range(QF):
                    g, which, half = f // 4, f // 2 % 2, f % 2
                    act.wait_ge(qk_done, at(b, QF, f + 1))
                    act.activation(staged(g)[:, 2 * which, half * BANK:(half + 1) * BANK].bitcast(F32R),
                                   psum[:, f % 4, :], ACT.Identity, bias=b_cols[:, which, g:g + 1]) \
                       .then_inc(qk_hi_ready, 1)

                def take_even(i):
                    s, hh = divmod(i, HG)
                    if hh == 0:
                        if s >= 2:
                            act.wait_ge(av_done, at(b, SETS, s - 1))
                        if s < GROUPS:
                            for head in range(HG * s, HG * (s + 1)):
                                act.wait_ge(parts_placed[head], 16 * 8 * b + 16 * 8)
                    act.wait_ge(turned, at(b, 2 * STEPS, 2 * i + 1))
                    act.activation(probsT_of(s)[:, hh, 0:TPH, :].rearrange("p k q -> p (k q)"),
                                   psum[:, T_BANK + 2 * i % T_RING, :], ACT.Copy).then_inc(even_taken, 1)

                def exponentiate(i):
                    act.wait_ge(masked, at(b, STEPS, i + 1))
                    if i >= 2:
                        act.wait_ge(turned, at(b, 2 * STEPS, 2 * (i - 1)))
                    act.activation(probs[:, i % 2], slot(i), ACT.Exp, bias=far[:, i:i + 1], scale=-1.0,
                                   accum_out=sums[:, i // HG, i % HG:i % HG + 1]).then_inc(probs_ready, 1)

                def take_recip(s):
                    act.wait_ge(recip_turned, at(b, SETS, s + 1))
                    if s >= 2:
                        act.wait_ge(o_ready, at(b, SETS, s - 1))
                    act.activation(recipT[:, s % 2], psum[:, O_BANK, P:2 * P], ACT.Copy) \
                       .then_inc(recipT_ready, 1)

                for i in range(STEPS + R_LAG - HG + 2):
                    if 0 <= i - T_LAG < STEPS:
                        take_even(i - T_LAG)
                    if i < STEPS:
                        exponentiate(i)
                    if i >= R_LAG and (i - R_LAG) % HG == 0:
                        take_recip((i - R_LAG) // HG)
                act.wait_ge(moments_ready, b + 1)
                act.activation(std[:], moments[:, :, 1], ACT.Sqrt, bias=eps[:, 0:1]).then_inc(std_ready, 1)

        @block.vector
        def _(dve):
            with dve.Fori(0, B) as b:
                for f in range(XF):
                    cols = slice((f % HALVES) * BANK, (f % HALVES + 1) * BANK)
                    dve.wait_ge(x1T_hi_ready, at(b, XF, f + 1))
                    dve.tensor_tensor(fT_lo[:, f // HALVES, cols], psum[:, 4 + f % 4, :],
                                      fT_hi[:, f // HALVES, cols].bitcast(F32), ALU.subtract) \
                       .then_inc(x1T_lo_ready, 1)
                for f in range(QF):
                    g, which, half = f // 4, f // 2 % 2, f % 2
                    cols = slice(half * BANK, (half + 1) * BANK)
                    dve.wait_ge(qk_hi_ready, at(b, QF, f + 1))
                    dve.scalar_tensor_tensor(out=staged(g)[:, 2 * which + 1, cols].bitcast(F32R),
                                             in0=psum[:, f % 4, :], scalar=b_cols[:, which, g:g + 1],
                                             in1=staged(g)[:, 2 * which, cols], op0=ALU.add, op1=ALU.subtract) \
                       .then_inc(qk_lo_ready, 1)
                for f in range(VF):
                    dve.wait_ge(v_done, at(b, VF, f + 1))
                    dve.tensor_tensor(v[:, 2 * f:2 * f + 2, :], psum[:, 4 + f, :].rearrange("p (t d) -> p t d", t=2),
                                      b_rows[:, 1:2, :].broadcast_to([P, 2, D]), ALU.add).then_inc(v_ready, 1)

                def add_mask(i):
                    dve.wait_ge(mask_ready, 1)
                    dve.wait_ge(scores_done, at(b, STEPS, i + 1))
                    dve.sem_inc(passed, 1)
                    dve.tensor_tensor_reduce(slot(i), slot(i), mask[:, i // HG % NT, :], 1.0, FAR, ALU.add, ALU.min,
                                             far[:, i:i + 1]).then_inc(masked, 1)

                def take_odd(i):
                    s, hh = divmod(i, HG)
                    if hh == 0:
                        if s >= 2:
                            dve.wait_ge(av_done, at(b, SETS, s - 1))
                        if s < GROUPS:
                            for head in range(HG * s, HG * (s + 1)):
                                dve.wait_ge(parts_placed[head], 16 * 8 * b + 16 * 8)
                    dve.wait_ge(turned, at(b, 2 * STEPS, 2 * i + 2))
                    dve.tensor_copy(probsT_of(s)[:, hh, TPH:NT, :].rearrange("p k q -> p (k q)"),
                                    psum[:, T_BANK + (2 * i + 1) % T_RING, :]).then_inc(odd_taken, 1)

                def reciprocals(s):
                    dve.wait_ge(probs_ready, at(b, STEPS, HG * (s + 1)))
                    dve.reciprocal(recip[:, s, :], sums[:, s, :]).then_inc(recip_ready, 1)

                def output(s):
                    cols = slice((s % NT) * P, (s % NT + 1) * P)
                    dve.wait_ge(recipT_ready, at(b, SETS, s + 1))
                    if s >= 2:
                        dve.wait_ge(o_lo_ready, at(b, SETS, s - 1))
                    dve.wait_ge(av_done, at(b, SETS, s + 1))
                    dve.tensor_tensor(o_full[:, s % 2], psum[:, O_BANK, 0:P], recipT[:, s % 2], ALU.mult)
                    dve.tensor_tensor(fT_hi[:, s // NT, cols], psum[:, O_BANK, 0:P], recipT[:, s % 2], ALU.mult) \
                       .then_inc(o_ready, 1)

                for i in range(STEPS + O_LAG - HG + 1):
                    if i >= O_LAG and (i - O_LAG) % HG == 0:
                        output((i - O_LAG) // HG)
                    if i < STEPS:
                        add_mask(i)
                    if i >= HG and i % HG == 0 and i // HG <= SETS:
                        reciprocals(i // HG - 1)
                    if 0 <= i - T_LAG < STEPS:
                        take_odd(i - T_LAG)

                dve.wait_ge(res_ready, b + 1)
                for f in range(VF):
                    h2 = h[:, 2 * f:2 * f + 2, :]
                    dve.wait_ge(proj_done, at(b, VF, f + 1))
                    dve.tensor_tensor(h2, psum[:, f, :].rearrange("p (t d) -> p t d", t=2), h2, ALU.add) \
                       .then_inc(h_ready, 1)
                for t in range(NT):
                    dve.wait_ge(h_ready, at(b, VF, t // 2 + 1))
                    dve.bn_stats(stats[:, t, :], h[:, t, :]).then_inc(stats_ready, 1)
                dve.wait_ge(stats_ready, at(b, NT, NT))
                dve.sem_inc(passed, 1)
                for t in range(NT):
                    ins = dve.bn_aggr(moments[:, t, :], stats[:, t, :])
                ins.then_inc(moments_ready, 1)
                dve.wait_ge(std_ready, b + 1)
                dve.reciprocal(rstd[:], std[:]).then_inc(rstd_ready, 1)
                dve.wait_ge(rstd_ready, b + 1)
                for t in range(NT):
                    ins = dve.tensor_scalar(h[:, t, :], h[:, t, :], moments[:, t, 0:1], rstd[:, t:t + 1],
                                            ALU.subtract, ALU.mult)
                ins.then_inc(normed, 1)

        @block.tensor
        def _(pe):
            with pe.Fori(0, B) as b:
                pe.wait_ge(x1_loaded, 16 * b + 16)
                for f in range(XF):
                    dc, half = divmod(f, HALVES)
                    for t in range(TPH):
                        ins = pe.transpose(psum[:, 4 + f % 4, t * P:(t + 1) * P],
                                           x1[:, half * TPH + t, dc * P:(dc + 1) * P], ident[:])
                    ins.then_inc(x1_turned, 1)
                pe.wait_ge(x1T_lo_ready, at(b, XF, XF))
                for f in range(QF):
                    g, which, half = f // 4, f // 2 % 2, f % 2
                    if f >= 4:
                        pe.wait_ge(qk_lo_ready, at(b, QF, f - 3))
                    outs, cols = slice(g * P, (g + 1) * P), slice(half * BANK, (half + 1) * BANK)
                    for dc in range(DC):
                        terms = split_terms(w_hi[:, WQ + which, dc, outs], w_lo[:, WQ + which, dc, outs],
                                            fT_hi[:, dc, cols], fT_lo[:, dc, cols])
                        for n, (lhsT, rhs) in enumerate(terms):
                            ins = pe.matmul(psum[:, f % 4, :], lhsT, rhs, start=(dc == 0 and n == 0),
                                            stop=(dc == DC - 1 and n == 2))
                    ins.then_inc(qk_done, 1)

                def rows_by_weight(bank, f, w):
                    for t in range(2):
                        cols = slice((2 * f + t) * P, (2 * f + t + 1) * P)
                        for dc in range(DC):
                            terms = split_terms(fT_hi[:, dc, cols], fT_lo[:, dc, cols], w_hi[:, w, dc], w_lo[:, w, dc])
                            for n, (lhsT, rhs) in enumerate(terms):
                                ins = pe.matmul(psum[:, bank, t * D:(t + 1) * D], lhsT, rhs,
                                                start=(dc == 0 and n == 0), stop=(dc == DC - 1 and n == 2))
                    return ins

                for f in range(VF):
                    rows_by_weight(4 + f, f, WV).then_inc(v_done, 1)

                def score(i):
                    s, hh = divmod(i, HG)
                    head, qt = HG * (s // NT) + hh, s % NT
                    if i % (HG * NT) < HG:
                        pe.wait_ge(parts_placed[head], 16 * 8 * b + 16 * 8)
                    if i < 2:
                        pe.wait_ge(qk_lo_ready, at(b, QF, QF))
                    else:
                        pe.wait_ge(probs_ready, at(b, STEPS, i - 1))
                    for half in range(HALVES):
                        ins = pe.matmul(psum[:, 2 * (i % 2) + half, :], q_parts[:, head, qt * P:(qt + 1) * P],
                                        k_parts[:, head, half * BANK:(half + 1) * BANK], start=True, stop=True)
                    ins.then_inc(scores_done, 1)

                def turn(i):
                    pe.wait_ge(probs_ready, at(b, STEPS, i + 1))
                    for half in range(2):
                        n = 2 * i + half
                        if n < T_RING:
                            pe.wait_ge(v_ready, at(b, VF, VF))
                        elif (n - T_RING) % 2:
                            pe.wait_ge(odd_taken, at(b, STEPS, (n - T_RING) // 2 + 1))
                        else:
                            pe.wait_ge(even_taken, at(b, STEPS, (n - T_RING) // 2 + 1))
                        for t in range(TPH):
                            kt = half * TPH + t
                            ins = pe.transpose(psum[:, T_BANK + n % T_RING, t * P:(t + 1) * P],
                                               probs[:, i % 2, kt * P:(kt + 1) * P], ident[:])
                        ins.then_inc(turned, 1)

                def turn_recip(s):
                    pe.wait_ge(wide_ready, at(b, SETS, s + 1))
                    if s >= 1:
                        pe.wait_ge(o_ready, at(b, SETS, s))
                    pe.transpose(psum[:, O_BANK, P:2 * P], recip_wide[:, s % 2].rearrange("p h d -> p (h d)"),
                                 ident[:]).then_inc(recip_turned, 1)

                def attend(s, part):
                    if part == 0:
                        pe.wait_ge(recipT_ready, at(b, SETS, s + 1))
                        pe.wait_ge(even_taken, at(b, STEPS, HG * (s + 1)))
                        pe.wait_ge(odd_taken, at(b, STEPS, HG * (s + 1)))
                    tiles = range(NT)[part * NT // AV_STEPS:(part + 1) * NT // AV_STEPS]
                    for kt in tiles:
                        for hh in range(HG):
                            head = HG * (s // NT) + hh
                            ins = pe.matmul(psum[hh * HD:(hh + 1) * HD, O_BANK, 0:P],
                                            v[:, kt, head * HD:(head + 1) * HD], probsT_of(s)[:, hh, kt, :],
                                            start=(kt == 0), stop=(kt == NT - 1))
                    if part == AV_STEPS - 1:
                        ins.then_inc(av_done, 1)

                for i in range(STEPS + O_LAG - HG):
                    if i < STEPS:
                        score(i)
                    if 0 <= i - T_LAG < STEPS:
                        turn(i - T_LAG)
                    if i >= R_LAG and (i - R_LAG) % HG == 0:
                        turn_recip((i - R_LAG) // HG)
                    elif i > R_LAG:
                        attend((i - R_LAG - 1) // HG, (i - R_LAG - 1) % HG)

                pe.wait_ge(o_lo_ready, at(b, SETS, SETS))
                for f in range(VF):
                    rows_by_weight(f, f, WO).then_inc(proj_done, 1)


_INS = ["x", "adj", "L0_gnn_weight", "L0_gnn_bias", "L1_gnn_Wq", "L1_gnn_bq", "L1_gnn_Wk", "L1_gnn_bk",
        "L1_gnn_Wv", "L1_gnn_bv", "L1_gnn_Wo", "L1_gnn_bo"]


def kernel(**inputs):
    import numpy as np
    import concourse.bacc as bacc
    from concourse.bass_utils import run_bass_kernel_spmd

    nc = bacc.Bacc("TRN2", target_bir_lowering=False, num_devices=1)
    arrays, aps = {}, {}
    for name in _INS:
        a = np.ascontiguousarray(inputs[name])
        arrays[f"in_{name}"] = a
        aps[name] = nc.dram_tensor(f"in_{name}", a.shape, mybir.dt.from_np(a.dtype), kind="ExternalInput").ap()
    out = nc.dram_tensor("out", arrays["in_x"].shape, F32, kind="ExternalOutput").ap()
    weights = [aps[n] for n in ("L0_gnn_weight", "L1_gnn_Wq", "L1_gnn_Wk", "L1_gnn_Wv", "L1_gnn_Wo")]
    biases = [aps[n] for n in ("L0_gnn_bias", "L1_gnn_bq", "L1_gnn_bk", "L1_gnn_bv", "L1_gnn_bo")]
    build(nc, aps["x"], aps["adj"], weights, biases, out)
    result = run_bass_kernel_spmd(nc, [arrays], core_ids=[0])
    return result.results[0]["out"]
```

```python
from contextlib import ExitStack

import concourse.bass as bass
from concourse import mybir

F32 = mybir.dt.float32
F32R = mybir.dt.float32r
ALU = mybir.AluOpType
ACT = mybir.ActivationFunctionType

P = 128
BANK = 512
HEADS = 8
EPS = 1e-5
MASKED = 1.0e9
FAR = 3.0e38
WQ, WK, WV, WO, W0 = range(5)


def split_terms(hi_a, lo_a, hi_b, lo_b):
    return ((hi_a, hi_b), (lo_a, hi_b), (hi_a, lo_b))


def build(nc, x, adj, weights, biases, out):
    B, N, D = x.shape
    NT = N // P
    DC = D // P
    HALVES = N // BANK
    TPH = BANK // P
    HD = D // HEADS
    HG = P // HD
    GROUPS = HEADS // HG
    SCALE = float(HD) ** -0.5
    x1_dram = nc.dram_tensor("x1_rows", (B, N, D), F32, kind="Internal").ap()

    with ExitStack() as whole:
        def sb(ctx, name, shape, dt=F32):
            return ctx.enter_context(nc.sbuf_tensor(name, shape, dt))

        def sem(ctx, name):
            return ctx.enter_context(nc.semaphore(name))

        psum = whole.enter_context(nc.psum_tensor("psum", [P, 8, BANK], F32))
        ident = sb(whole, "ident", [P, P])
        mask = sb(whole, "mask", [P, NT, N])
        w_hi = sb(whole, "w_hi", [P, 4, DC, D], F32R)
        w_lo = sb(whole, "w_lo", [P, 4, DC, D], F32R)
        b_rows = sb(whole, "b_rows", [P, 3, D])
        b_cols = sb(whole, "b_cols", [P, 2, GROUPS])
        b_in = sb(whole, "b_in", [P, 2, GROUPS])
        eps = sb(whole, "eps", [P, 1])
        mask_ready = sem(whole, "mask_ready")

        layer_norm_1(nc, sb, sem, x, adj, weights, biases, x1_dram, psum, ident, mask, w_hi, w_lo,
                     b_rows, b_cols, b_in, eps, mask_ready, (B, N, D, NT, DC, HALVES, TPH, GROUPS, SCALE))
        layer_norm_2(nc, sb, sem, x1_dram, out, psum, ident, mask, w_hi, w_lo, b_rows, b_cols, eps,
                     mask_ready, (B, N, D, NT, DC, HALVES, TPH, HD, HG, GROUPS))


def layer_norm_1(nc, sb, sem, x, adj, weights, biases, x1_dram, psum, ident, mask, w_hi, w_lo,
                 b_rows, b_cols, b_in, eps, mask_ready, sizes):
    B, N, D, NT, DC, HALVES, TPH, GROUPS, SCALE = sizes
    CH = HALVES * DC
    HB = NT // 2
    PAIRS = B // 2
    with ExitStack() as ctx:
        adjT_hi = sb(ctx, "adjT_hi", [P, NT, N], F32R)
        adjT_lo = sb(ctx, "adjT_lo", [P, NT, N], F32R)
        xin = sb(ctx, "xin", [P, 2, NT, D])
        x_hi = sb(ctx, "x_hi", [P, 2, NT, D], F32R)
        x_lo = sb(ctx, "x_lo", [P, 2, NT, D], F32R)
        yT_hi = sb(ctx, "yT_hi", [P, DC, N], F32R)
        yT_lo = sb(ctx, "yT_lo", [P, DC, N], F32R)
        w_in = sb(ctx, "w_in", [P, 5, DC, D])
        w0_hi = sb(ctx, "w0_hi", [P, DC, D], F32R)
        w0_lo = sb(ctx, "w0_lo", [P, DC, D], F32R)
        stats = sb(ctx, "stats", [P, NT, 6])
        moments = sb(ctx, "moments", [P, NT, 2])
        std = sb(ctx, "std", [P, NT])
        rstd = sb(ctx, "rstd", [P, NT])

        adj_loaded = [sem(ctx, f"adj_loaded{h}") for h in range(HALVES)]
        w_loaded = sem(ctx, "w_loaded")
        b_loaded = sem(ctx, "b_loaded")
        x_loaded = [sem(ctx, f"x_loaded{u}") for u in range(2)]
        x1_stored = [sem(ctx, f"x1_stored{u}") for u in range(2)]
        zeroed = sem(ctx, "zeroed")
        ident_ready = sem(ctx, "ident_ready")
        eps_ready = sem(ctx, "eps_ready")
        wq_scaled = sem(ctx, "wq_scaled")
        w_hi_ready = sem(ctx, "w_hi_ready")
        w_lo_ready = sem(ctx, "w_lo_ready")
        adj_turned = sem(ctx, "adj_turned")
        adjT_hi_ready = sem(ctx, "adjT_hi_ready")
        adjT_lo_ready = sem(ctx, "adjT_lo_ready")
        x_hi_ready = sem(ctx, "x_hi_ready")
        x_lo_ready = sem(ctx, "x_lo_ready")
        xb_ready = sem(ctx, "xb_ready")
        yT_done = sem(ctx, "yT_done")
        yT_hi_ready = sem(ctx, "yT_hi_ready")
        yT_lo_ready = sem(ctx, "yT_lo_ready")
        h_done = sem(ctx, "h_done")
        h_ready = sem(ctx, "h_ready")
        stats_ready = sem(ctx, "stats_ready")
        moments_ready = sem(ctx, "moments_ready")
        std_ready = sem(ctx, "std_ready")
        rstd_ready = sem(ctx, "rstd_ready")
        x1_ready = sem(ctx, "x1_ready")
        passed = sem(ctx, "passed")

        def rows(dram, b):
            return dram[b].rearrange("(t p) d -> p t d", p=P)

        block = ctx.enter_context(nc.Block())

        @block.sync
        def _(sp):
            adj_rows = adj.rearrange("(t p) m -> p t m", p=P)
            for h in range(HALVES):
                sp.dma_start(mask[:, h * TPH:(h + 1) * TPH, :], adj_rows[:, h * TPH:(h + 1) * TPH, :]) \
                  .then_inc(adj_loaded[h], 16)
                sp.dma_start(xin[:, h], rows(x, h)).then_inc(x_loaded[h], 16)
            for i, w in enumerate((*weights[1:], weights[0])):
                sp.dma_start(w_in[:, i], w.rearrange("(c p) n -> p c n", p=P)).then_inc(w_loaded, 16)
            for i, v in enumerate((biases[0], biases[3], biases[4])):
                sp.dma_start(b_rows[:, i, :], v.rearrange("(a d) -> a d", a=1).broadcast_to([P, D])) \
                  .then_inc(b_loaded, 16)
            with nc.allow_non_contiguous_dma(reason="one feature per partition"):
                for i in range(2):
                    sp.dma_start(b_in[:, i, :], biases[1 + i].rearrange("(g p) -> p g", p=P)) \
                      .then_inc(b_loaded, 16)

            def store(b, j, u):
                sp.wait_ge(x1_ready, b + 1)
                sp.dma_start(rows(x1_dram, b), xin[:, u]).then_inc(x1_stored[u], 16)

            with sp.Fori(0, PAIRS - 1) as j:
                for u in range(2):
                    store(2 * j + u, j, u)
                    sp.wait_ge(x1_stored[u], 16 * j + 16)
                    sp.dma_start(xin[:, u], rows(x, 2 * j + u + 2)).then_inc(x_loaded[u], 16)
            for u in range(2):
                store(B - 2 + u, PAIRS - 1, u)
            for u in range(2):
                sp.wait_ge(x1_stored[u], 16 * PAIRS)

        @block.gpsimd
        def _(pool):
            pool.memset(ident[:], 0.0).then_inc(zeroed, 1)
            pool.wait_ge(zeroed, 1)
            pool.affine_select(out=ident[:], in_=ident[:], compare_op=ALU.not_equal, fill=1.0, base=0,
                               pattern=[[-1, P]], channel_multiplier=1).then_inc(ident_ready, 1)
            pool.memset(eps[:], EPS).then_inc(eps_ready, 1)

            def x_parts(b, j, u):
                pool.wait_ge(x_hi_ready, b + 1)
                pool.tensor_tensor(x_lo[:, u], xin[:, u], x_hi[:, u].bitcast(F32), ALU.subtract) \
                    .then_inc(x_lo_ready, 1)
                pool.tensor_tensor(xin[:, u], xin[:, u],
                                   b_rows[:, 0:1, :].broadcast_to([P, NT, D]), ALU.add).then_inc(xb_ready, 1)

            pool.wait_ge(w_hi_ready, 2)
            pool.wait_ge(wq_scaled, 2)
            pool.tensor_tensor(w0_lo[:], w_in[:, W0], w0_hi[:].bitcast(F32), ALU.subtract).then_inc(w_lo_ready, 1)
            pool.tensor_tensor(w_lo[:], w_in[:, 0:4], w_hi[:].bitcast(F32), ALU.subtract).then_inc(w_lo_ready, 1)
            pool.wait_ge(b_loaded, 16 * 5)
            with pool.Fori(0, PAIRS) as j:
                for u in range(2):
                    x_parts(2 * j + u, j, u)

        @block.scalar
        def _(act):
            def x_high(b, j, u):
                act.wait_ge(x_loaded[u], 16 * j + 16)
                act.activation(x_hi[:, u], xin[:, u], ACT.Copy).then_inc(x_hi_ready, 1)

            x_high(0, 0, 0)
            act.wait_ge(wq_scaled, 2)
            act.activation(w_hi[:], w_in[:, 0:4], ACT.Copy).then_inc(w_hi_ready, 1)
            act.activation(w0_hi[:], w_in[:, W0], ACT.Copy).then_inc(w_hi_ready, 1)
            for f in range(HALVES * NT):
                act.wait_ge(adj_turned, f + 1)
                act.activation(adjT_hi[:, f % NT, (f // NT) * BANK:(f // NT + 1) * BANK], psum[:, f % 8, :],
                               ACT.Copy).then_inc(adjT_hi_ready, 1)

            def batch(b, j, u, last):
                for c in range(CH):
                    h, dc = divmod(c, DC)
                    act.wait_ge(yT_done, CH * b + c + 1)
                    act.activation(yT_hi[:, dc, h * BANK:(h + 1) * BANK], psum[:, c, :],
                                   ACT.Copy).then_inc(yT_hi_ready, 1)
                    if c == CH - 2 and not last:
                        x_high(b + 1, j + u, 1 - u)
                act.wait_ge(moments_ready, b + 1)
                act.activation(std[:], moments[:, :, 1], ACT.Sqrt, bias=eps[:, 0:1]).then_inc(std_ready, 1)

            act.wait_ge(eps_ready, 1)
            with act.Fori(0, PAIRS - 1) as j:
                for u in range(2):
                    batch(2 * j + u, j, u, False)
            for u in range(2):
                batch(B - 2 + u, PAIRS - 1, u, u == 1)

        @block.vector
        def _(dve):
            dve.wait_ge(w_loaded, 16 * 5)
            dve.tensor_scalar(w_in[:, WQ], w_in[:, WQ], -SCALE, None, ALU.mult).then_inc(wq_scaled, 1)
            dve.wait_ge(b_loaded, 16 * 5)
            dve.tensor_scalar(b_cols[:, 0, :], b_in[:, 0, :], -SCALE, None, ALU.mult).then_inc(wq_scaled, 1)
            dve.tensor_copy(b_cols[:, 1, :], b_in[:, 1, :]).then_inc(wq_scaled, 1)
            for f in range(HALVES * NT):
                dve.wait_ge(adjT_hi_ready, f + 1)
                cols = slice((f // NT) * BANK, (f // NT + 1) * BANK)
                dve.tensor_tensor(adjT_lo[:, f % NT, cols], psum[:, f % 8, :],
                                  adjT_hi[:, f % NT, cols].bitcast(F32), ALU.subtract).then_inc(adjT_lo_ready, 1)
            dve.wait_ge(adj_turned, HALVES * NT)
            dve.tensor_scalar(mask[:], mask[:], 1.0, -MASKED, ALU.subtract, ALU.mult).then_inc(mask_ready, 1)

            def batch(b, j, u):
                for c in range(CH):
                    h, dc = divmod(c, DC)
                    cols = slice(h * BANK, (h + 1) * BANK)
                    dve.wait_ge(yT_hi_ready, CH * b + c + 1)
                    dve.tensor_tensor(yT_lo[:, dc, cols], psum[:, c, :], yT_hi[:, dc, cols].bitcast(F32),
                                      ALU.subtract).then_inc(yT_lo_ready, 1)
                dve.wait_ge(xb_ready, b + 1)
                for w in range(HB):
                    h2 = xin[:, u, 2 * w:2 * w + 2, :]
                    dve.wait_ge(h_done, HB * b + w + 1)
                    dve.tensor_tensor(h2, psum[:, 4 + w, :].rearrange("p (t d) -> p t d", t=2), h2, ALU.add) \
                       .then_inc(h_ready, 1)
                for t in range(NT):
                    dve.wait_ge(h_ready, HB * b + t // 2 + 1)
                    dve.bn_stats(stats[:, t, :], xin[:, u, t, :]).then_inc(stats_ready, 1)
                dve.wait_ge(stats_ready, NT * b + NT)
                dve.sem_inc(passed, 1)
                for t in range(NT):
                    ins = dve.bn_aggr(moments[:, t, :], stats[:, t, :])
                ins.then_inc(moments_ready, 1)
                dve.wait_ge(std_ready, b + 1)
                dve.reciprocal(rstd[:], std[:]).then_inc(rstd_ready, 1)
                dve.wait_ge(rstd_ready, b + 1)
                for t in range(NT):
                    ins = dve.tensor_scalar(xin[:, u, t, :], xin[:, u, t, :], moments[:, t, 0:1],
                                            rstd[:, t:t + 1], ALU.subtract, ALU.mult)
                ins.then_inc(x1_ready, 1)

            with dve.Fori(0, PAIRS) as j:
                for u in range(2):
                    batch(2 * j + u, j, u)

        @block.tensor
        def _(pe):
            pe.wait_ge(ident_ready, 1)
            for h in range(HALVES):
                pe.wait_ge(adj_loaded[h], 16)
                for mt in range(NT):
                    f = h * NT + mt
                    if f >= 8:
                        pe.wait_ge(adjT_lo_ready, f - 7)
                    for t in range(TPH):
                        ins = pe.transpose(psum[:, f % 8, t * P:(t + 1) * P],
                                           mask[:, h * TPH + t, mt * P:(mt + 1) * P], ident[:])
                    ins.then_inc(adj_turned, 1)
            pe.wait_ge(adjT_lo_ready, HALVES * NT)
            pe.wait_ge(w_lo_ready, 2)

            def chunk(b, u, c):
                h, dc = divmod(c, DC)
                for mt in range(NT):
                    cols = slice(h * BANK, (h + 1) * BANK)
                    terms = split_terms(x_hi[:, u, mt, dc * P:(dc + 1) * P], x_lo[:, u, mt, dc * P:(dc + 1) * P],
                                        adjT_hi[:, mt, cols], adjT_lo[:, mt, cols])
                    for n, (lhsT, rhs) in enumerate(terms):
                        ins = pe.matmul(psum[:, c, :], lhsT, rhs, start=(mt == 0 and n == 0),
                                        stop=(mt == NT - 1 and n == 2))
                ins.then_inc(yT_done, 1)

            def project(b, w):
                for t in range(2):
                    cols = slice((2 * w + t) * P, (2 * w + t + 1) * P)
                    for dc in range(DC):
                        terms = split_terms(yT_hi[:, dc, cols], yT_lo[:, dc, cols], w0_hi[:, dc], w0_lo[:, dc])
                        for n, (lhsT, rhs) in enumerate(terms):
                            ins = pe.matmul(psum[:, 4 + w, t * D:(t + 1) * D], lhsT, rhs,
                                            start=(dc == 0 and n == 0), stop=(dc == DC - 1 and n == 2))
                ins.then_inc(h_done, 1)

            def batch(b, j, u):
                pe.wait_ge(x_lo_ready, b + 1)
                for c in range(CH - 1):
                    chunk(b, u, c)
                pe.wait_ge(yT_lo_ready, CH * b + DC)
                for w in range(HB // 2):
                    project(b, w)
                chunk(b, u, CH - 1)
                pe.wait_ge(yT_lo_ready, CH * b + CH)
                for w in range(HB // 2, HB):
                    project(b, w)

            with pe.Fori(0, PAIRS) as j:
                for u in range(2):
                    batch(2 * j + u, j, u)


def layer_norm_2(nc, sb, sem, x1_dram, out, psum, ident, mask, w_hi, w_lo, b_rows, b_cols, eps,
                 mask_ready, sizes):
    B, N, D, NT, DC, HALVES, TPH, HD, HG, GROUPS = sizes
    XF = DC * HALVES
    QF = GROUPS * 2 * HALVES
    VF = NT // 2
    STEPS = HEADS * NT
    SETS = GROUPS * NT
    PARTS = 3
    PLACED = 16 * 2 * PARTS
    T_LAG = 2
    R_LAG = HG - 1 + T_LAG
    AV_LAG = R_LAG + 1
    O_LAG = AV_LAG + HG
    UNITS = 2 * HG + 1
    T_BANK, T_RING = 4, 3
    O_BANK = 7
    with ExitStack() as ctx:
        x1 = sb(ctx, "x1", [P, NT, D])
        h = sb(ctx, "h", [P, NT, D])
        fT_hi = sb(ctx, "fT_hi", [P, DC, N], F32R)
        fT_lo = sb(ctx, "fT_lo", [P, DC, N], F32R)
        q_parts = sb(ctx, "q_parts", [P, HEADS, N], F32R)
        k_parts = sb(ctx, "k_parts", [P, HEADS, N], F32R)
        v = sb(ctx, "v", [P, NT, D])
        probs = sb(ctx, "probs", [P, 2, N])
        probsT = sb(ctx, "probsT", [P, 2, HG * N])
        q1_staged = sb(ctx, "q1_staged", [P, 2, N])
        far = sb(ctx, "far", [P, STEPS])
        sums = sb(ctx, "sums", [P, SETS, HG])
        recip = sb(ctx, "recip", [P, SETS, HG])
        ones = sb(ctx, "ones", [P, HD])
        recip_wide = sb(ctx, "recip_wide", [P, 2, HG, HD])
        recipT = sb(ctx, "recipT", [P, 2, P])
        o_full = sb(ctx, "o_full", [P, 2, P])
        stats = sb(ctx, "stats2", [P, NT, 6])
        moments = sb(ctx, "moments2", [P, NT, 2])
        std = sb(ctx, "std2", [P, NT])
        rstd = sb(ctx, "rstd2", [P, NT])
        shift = sb(ctx, "shift", [P, NT])

        x1_loaded = sem(ctx, "x1_loaded")
        res_loaded = sem(ctx, "res_loaded")
        stored = sem(ctx, "stored")
        ones_ready = sem(ctx, "ones_ready")
        res_ready = sem(ctx, "res_ready")
        x1_turned = sem(ctx, "x1_turned")
        x1T_hi_ready = sem(ctx, "x1T_hi_ready")
        x1T_lo_ready = sem(ctx, "x1T_lo_ready")
        qk_done = sem(ctx, "qk_done")
        qk_hi_ready = sem(ctx, "qk_hi_ready")
        qk_lo_ready = sem(ctx, "qk_lo_ready")
        parts_placed = [sem(ctx, f"parts_placed{i}") for i in range(HEADS)]
        v_done = sem(ctx, "v_done")
        v_ready = sem(ctx, "v_ready")
        scores_done = sem(ctx, "scores_done")
        masked = sem(ctx, "masked")
        probs_ready = sem(ctx, "probs_ready")
        turned = sem(ctx, "turned")
        even_taken = sem(ctx, "even_taken")
        odd_taken = sem(ctx, "odd_taken")
        recip_ready = sem(ctx, "recip_ready")
        wide_ready = sem(ctx, "wide_ready")
        recip_turned = sem(ctx, "recip_turned")
        recipT_ready = sem(ctx, "recipT_ready")
        av_done = sem(ctx, "av_done")
        o_ready = sem(ctx, "o_ready")
        o_lo_ready = sem(ctx, "o_lo_ready")
        proj_done = sem(ctx, "proj_done")
        h_ready = sem(ctx, "h_ready2")
        stats_ready = sem(ctx, "stats_ready2")
        moments_ready = sem(ctx, "moments_ready2")
        std_ready = sem(ctx, "std_ready2")
        rstd_ready = sem(ctx, "rstd_ready2")
        shift_ready = sem(ctx, "shift_ready")
        normed = sem(ctx, "normed")
        passed = sem(ctx, "passed2")

        def rows(dram, b):
            return dram[b].rearrange("(t p) d -> p t d", p=P)

        def staged(g, which):
            if g == 0:
                return probsT[:, 1, 2 * which * N:2 * (which + 1) * N].rearrange("p (w n) -> p w n", w=2)
            return x1[:].rearrange("p (w t) d -> p w (t d)", w=2) if which else q1_staged[:]

        def probsT_of(g):
            return probsT[:, g % 2, :].rearrange("p (h k q) -> p h k q", h=HG, k=NT)

        def slot(i):
            return psum[:, 2 * (i % 2):2 * (i % 2) + 2, :].rearrange("p a n -> p (a n)")

        def turn_bank(unit):
            return T_BANK + unit % T_RING

        def unit_of(i, half):
            return UNITS * (i // HG) + 2 * (i % HG) + half

        def at(b, per, n):
            assert n > 0
            return b * per + n

        block = ctx.enter_context(nc.Block())

        @block.sync
        def _(sp):
            def place(b, g):
                for which, parts, order in ((0, q_parts, (0, 1, 0)), (1, k_parts, (0, 0, 1))):
                    sp.wait_ge(qk_lo_ready, at(b, QF, HALVES * (2 * g + which + 1)))
                    for hh in range(HG):
                        own = slice(hh * HD, (hh + 1) * HD)
                        for r, part in enumerate(order):
                            sp.dma_start(parts[r * HD:(r + 1) * HD, HG * g + hh, :].bitcast(F32),
                                         staged(g, which)[own, part, :]) \
                              .then_inc(parts_placed[HG * g + hh], 16)

            def residual(b):
                sp.dma_start(h[:], rows(x1_dram, b)).then_inc(res_loaded, 16)

            def result(b):
                sp.wait_ge(normed, b + 1)
                sp.dma_start(rows(out, b), h[:]).then_inc(stored, 16)

            sp.dma_start(x1[:], rows(x1_dram, 0)).then_inc(x1_loaded, 16)
            residual(0)
            with sp.Fori(0, B - 1) as b:
                place(b, 0)
                place(b, 1)
                for head in range(HG, HEADS):
                    sp.wait_ge(parts_placed[head], PLACED * b + PLACED)
                sp.dma_start(x1[:], rows(x1_dram, b + 1)).then_inc(x1_loaded, 16)
                result(b)
                sp.wait_ge(stored, 16 * b + 16)
                residual(b + 1)
            place(B - 1, 0)
            place(B - 1, 1)
            result(B - 1)
            sp.wait_ge(stored, 16 * B)

        @block.gpsimd
        def _(pool):
            pool.memset(ones[:], 1.0).then_inc(ones_ready, 1)
            pool.wait_ge(ones_ready, 1)
            with pool.Fori(0, B) as b:
                pool.wait_ge(res_loaded, 16 * b + 16)
                pool.tensor_tensor(h[:], h[:], b_rows[:, 2:3, :].broadcast_to([P, NT, D]), ALU.add) \
                    .then_inc(res_ready, 1)

                def widen(s):
                    pool.wait_ge(recip_ready, at(b, SETS, s + 1))
                    if s >= 2:
                        pool.wait_ge(recip_turned, at(b, SETS, s - 1))
                    pool.tensor_tensor(recip_wide[:, s % 2], recip[:, s, :].rearrange("p (h a) -> p h a", a=1)
                                       .broadcast_to([P, HG, HD]),
                                       ones[:].rearrange("p (a d) -> p a d", a=1).broadcast_to([P, HG, HD]),
                                       ALU.mult).then_inc(wide_ready, 1)

                def o_low(s):
                    cols = slice((s % NT) * P, (s % NT + 1) * P)
                    pool.wait_ge(o_ready, at(b, SETS, s + 1))
                    pool.tensor_tensor(fT_lo[:, s // NT, cols], o_full[:, s % 2],
                                       fT_hi[:, s // NT, cols].bitcast(F32), ALU.subtract) \
                        .then_inc(o_lo_ready, 1)

                for s in range(SETS + 1):
                    if s < SETS:
                        widen(s)
                    if s >= 1:
                        o_low(s - 1)
                pool.wait_ge(shift_ready, b + 1)
                pool.sem_inc(passed, 1)
                for t in range(NT):
                    ins = pool.tensor_scalar(h[:, t, :], h[:, t, :], rstd[:, t:t + 1], shift[:, t:t + 1],
                                             ALU.mult, ALU.add)
                ins.then_inc(normed, 1)

        @block.scalar
        def _(act):
            with act.Fori(0, B) as b:
                for f in range(XF):
                    act.wait_ge(x1_turned, at(b, XF, f + 1))
                    act.activation(fT_hi[:, f % DC, (f // DC) * BANK:(f // DC + 1) * BANK],
                                   psum[:, 4 + f % 4, :], ACT.Copy).then_inc(x1T_hi_ready, 1)
                for f in range(QF):
                    g, which, half = f // 4, f // 2 % 2, f % 2
                    act.wait_ge(qk_done, at(b, QF, f + 1))
                    act.activation(staged(g, which)[:, 0, half * BANK:(half + 1) * BANK].bitcast(F32R),
                                   psum[:, f % 4, :], ACT.Identity, bias=b_cols[:, which, g:g + 1]) \
                       .then_inc(qk_hi_ready, 1)

                def take_even(i):
                    s, hh = divmod(i, HG)
                    if hh == 0:
                        if s >= 2:
                            act.wait_ge(av_done, at(b, SETS, s - 1))
                        if s == 1:
                            for head in range(HG):
                                act.wait_ge(parts_placed[head], PLACED * b + PLACED)
                    act.wait_ge(turned, at(b, 2 * STEPS, 2 * i + 1))
                    act.activation(probsT_of(s)[:, hh, 0:TPH, :].rearrange("p k q -> p (k q)"),
                                   psum[:, turn_bank(unit_of(i, 0)), :], ACT.Copy).then_inc(even_taken, 1)

                def exponentiate(i):
                    act.wait_ge(masked, at(b, STEPS, i + 1))
                    if i >= 2:
                        act.wait_ge(turned, at(b, 2 * STEPS, 2 * (i - 1)))
                    act.activation(probs[:, i % 2], slot(i), ACT.Exp, bias=far[:, i:i + 1], scale=-1.0,
                                   accum_out=sums[:, i // HG, i % HG:i % HG + 1]).then_inc(probs_ready, 1)

                def take_recip(s):
                    act.wait_ge(recip_turned, at(b, SETS, s + 1))
                    if s >= 2:
                        act.wait_ge(o_ready, at(b, SETS, s - 1))
                    act.activation(recipT[:, s % 2], psum[:, turn_bank(UNITS * s + UNITS - 1), 0:P], ACT.Copy) \
                       .then_inc(recipT_ready, 1)

                for i in range(STEPS + T_LAG):
                    if 0 <= i - T_LAG < STEPS:
                        take_even(i - T_LAG)
                    if i < STEPS:
                        exponentiate(i)
                    if i % HG == R_LAG % HG and i >= R_LAG:
                        take_recip((i - R_LAG) // HG)
                act.wait_ge(moments_ready, b + 1)
                act.activation(std[:], moments[:, :, 1], ACT.Sqrt, bias=eps[:, 0:1]).then_inc(std_ready, 1)

        @block.vector
        def _(dve):
            with dve.Fori(0, B) as b:
                for f in range(XF):
                    cols = slice((f // DC) * BANK, (f // DC + 1) * BANK)
                    dve.wait_ge(x1T_hi_ready, at(b, XF, f + 1))
                    dve.tensor_tensor(fT_lo[:, f % DC, cols], psum[:, 4 + f % 4, :],
                                      fT_hi[:, f % DC, cols].bitcast(F32), ALU.subtract) \
                       .then_inc(x1T_lo_ready, 1)
                for f in range(QF):
                    g, which, half = f // 4, f // 2 % 2, f % 2
                    cols = slice(half * BANK, (half + 1) * BANK)
                    dve.wait_ge(qk_hi_ready, at(b, QF, f + 1))
                    dve.scalar_tensor_tensor(out=staged(g, which)[:, 1, cols].bitcast(F32R),
                                             in0=psum[:, f % 4, :], scalar=b_cols[:, which, g:g + 1],
                                             in1=staged(g, which)[:, 0, cols], op0=ALU.add, op1=ALU.subtract) \
                       .then_inc(qk_lo_ready, 1)
                for f in range(VF):
                    dve.wait_ge(v_done, at(b, VF, f + 1))
                    dve.tensor_tensor(v[:, 2 * f:2 * f + 2, :], psum[:, 4 + f, :].rearrange("p (t d) -> p t d", t=2),
                                      b_rows[:, 1:2, :].broadcast_to([P, 2, D]), ALU.add).then_inc(v_ready, 1)

                def add_mask(i):
                    dve.wait_ge(mask_ready, 1)
                    dve.wait_ge(scores_done, at(b, STEPS, i + 1))
                    dve.sem_inc(passed, 1)
                    dve.tensor_tensor_reduce(slot(i), slot(i), mask[:, i // HG % NT, :], 1.0, FAR, ALU.add, ALU.min,
                                             far[:, i:i + 1]).then_inc(masked, 1)

                def take_odd(i):
                    s, hh = divmod(i, HG)
                    if hh == 0:
                        if s >= 2:
                            dve.wait_ge(av_done, at(b, SETS, s - 1))
                        if s == 1:
                            for head in range(HG):
                                dve.wait_ge(parts_placed[head], PLACED * b + PLACED)
                    dve.wait_ge(turned, at(b, 2 * STEPS, 2 * i + 2))
                    dve.tensor_copy(probsT_of(s)[:, hh, TPH:NT, :].rearrange("p k q -> p (k q)"),
                                    psum[:, turn_bank(unit_of(i, 1)), :]).then_inc(odd_taken, 1)

                def reciprocals(s):
                    dve.wait_ge(probs_ready, at(b, STEPS, HG * (s + 1)))
                    dve.reciprocal(recip[:, s, :], sums[:, s, :]).then_inc(recip_ready, 1)

                def output(s):
                    cols = slice((s % NT) * P, (s % NT + 1) * P)
                    dve.wait_ge(recipT_ready, at(b, SETS, s + 1))
                    if s >= 2:
                        dve.wait_ge(o_lo_ready, at(b, SETS, s - 1))
                    dve.wait_ge(av_done, at(b, SETS, s + 1))
                    dve.tensor_tensor(o_full[:, s % 2], psum[:, O_BANK, 0:P], recipT[:, s % 2], ALU.mult)
                    dve.tensor_tensor(fT_hi[:, s // NT, cols], psum[:, O_BANK, 0:P], recipT[:, s % 2], ALU.mult) \
                       .then_inc(o_ready, 1)

                def residual(f):
                    h2 = h[:, 2 * f:2 * f + 2, :]
                    dve.wait_ge(proj_done, at(b, VF, f + 1))
                    dve.tensor_tensor(h2, psum[:, f, :].rearrange("p (t d) -> p t d", t=2), h2, ALU.add) \
                       .then_inc(h_ready, 1)
                    dve.wait_ge(h_ready, at(b, VF, f + 1))
                    for t in (2 * f, 2 * f + 1):
                        dve.bn_stats(stats[:, t, :], h[:, t, :]).then_inc(stats_ready, 1)

                for i in range(STEPS + T_LAG):
                    if i >= O_LAG and (i - O_LAG) % HG == 0:
                        output((i - O_LAG) // HG)
                    if i < STEPS:
                        add_mask(i)
                    if i % HG == 0 and i >= HG:
                        reciprocals(i // HG - 1)
                    if i >= T_LAG:
                        take_odd(i - T_LAG)
                    if i == STEPS:
                        dve.wait_ge(res_ready, b + 1)
                        output(SETS - 2)
                        residual(0)
                residual(1)
                residual(2)
                output(SETS - 1)
                for f in range(3, VF):
                    residual(f)
                dve.wait_ge(stats_ready, at(b, NT, NT))
                dve.sem_inc(passed, 1)
                for t in range(NT):
                    ins = dve.bn_aggr(moments[:, t, :], stats[:, t, :])
                ins.then_inc(moments_ready, 1)
                dve.wait_ge(std_ready, b + 1)
                dve.reciprocal(rstd[:], std[:]).then_inc(rstd_ready, 1)
                dve.wait_ge(rstd_ready, b + 1)
                dve.scalar_tensor_tensor(out=shift[:], in0=moments[:, :, 0], scalar=-1.0, in1=rstd[:],
                                         op0=ALU.mult, op1=ALU.mult).then_inc(shift_ready, 1)

        @block.tensor
        def _(pe):
            with pe.Fori(0, B) as b:
                pe.wait_ge(x1_loaded, 16 * b + 16)
                for f in range(XF):
                    half, dc = divmod(f, DC)
                    for t in range(TPH):
                        ins = pe.transpose(psum[:, 4 + f % 4, t * P:(t + 1) * P],
                                           x1[:, half * TPH + t, dc * P:(dc + 1) * P], ident[:])
                    ins.then_inc(x1_turned, 1)
                for f in range(QF):
                    g, which, half = f // 4, f // 2 % 2, f % 2
                    if f < HALVES:
                        pe.wait_ge(x1T_lo_ready, at(b, XF, DC * (f + 1)))
                    if f >= 4:
                        pe.wait_ge(qk_lo_ready, at(b, QF, f - 3))
                    outs, cols = slice(g * P, (g + 1) * P), slice(half * BANK, (half + 1) * BANK)
                    for dc in range(DC):
                        terms = split_terms(w_hi[:, WQ + which, dc, outs], w_lo[:, WQ + which, dc, outs],
                                            fT_hi[:, dc, cols], fT_lo[:, dc, cols])
                        for n, (lhsT, rhs) in enumerate(terms):
                            ins = pe.matmul(psum[:, f % 4, :], lhsT, rhs, start=(dc == 0 and n == 0),
                                            stop=(dc == DC - 1 and n == 2))
                    ins.then_inc(qk_done, 1)

                def rows_by_weight(bank, f, w):
                    for t in range(2):
                        cols = slice((2 * f + t) * P, (2 * f + t + 1) * P)
                        for dc in range(DC):
                            terms = split_terms(fT_hi[:, dc, cols], fT_lo[:, dc, cols], w_hi[:, w, dc], w_lo[:, w, dc])
                            for n, (lhsT, rhs) in enumerate(terms):
                                ins = pe.matmul(psum[:, bank, t * D:(t + 1) * D], lhsT, rhs,
                                                start=(dc == 0 and n == 0), stop=(dc == DC - 1 and n == 2))
                    return ins

                for f in range(VF):
                    rows_by_weight(4 + f, f, WV).then_inc(v_done, 1)

                def score(i):
                    s, hh = divmod(i, HG)
                    head, qt = HG * (s // NT) + hh, s % NT
                    if i % (HG * NT) < HG:
                        pe.wait_ge(parts_placed[head], PLACED * b + PLACED)
                    if i < 2:
                        pe.wait_ge(qk_lo_ready, at(b, QF, QF))
                    else:
                        pe.wait_ge(probs_ready, at(b, STEPS, i - 1))
                    for half in range(HALVES):
                        ins = pe.matmul(psum[:, 2 * (i % 2) + half, :], q_parts[0:PARTS * HD, head, qt * P:(qt + 1) * P],
                                        k_parts[0:PARTS * HD, head, half * BANK:(half + 1) * BANK], start=True, stop=True)
                    ins.then_inc(scores_done, 1)

                def wait_turn_bank(unit):
                    s, n = divmod(unit - T_RING, UNITS)
                    if unit < T_RING:
                        pe.wait_ge(v_ready, at(b, VF, VF))
                    elif n == UNITS - 1:
                        pe.wait_ge(recipT_ready, at(b, SETS, s + 1))
                    elif n % 2:
                        pe.wait_ge(odd_taken, at(b, STEPS, HG * s + n // 2 + 1))
                    else:
                        pe.wait_ge(even_taken, at(b, STEPS, HG * s + n // 2 + 1))

                def turn(i):
                    pe.wait_ge(probs_ready, at(b, STEPS, i + 1))
                    for half in range(2):
                        unit = unit_of(i, half)
                        wait_turn_bank(unit)
                        for t in range(TPH):
                            kt = half * TPH + t
                            ins = pe.transpose(psum[:, turn_bank(unit), t * P:(t + 1) * P],
                                               probs[:, i % 2, kt * P:(kt + 1) * P], ident[:])
                        ins.then_inc(turned, 1)

                def turn_recip(s):
                    pe.wait_ge(wide_ready, at(b, SETS, s + 1))
                    wait_turn_bank(UNITS * s + UNITS - 1)
                    pe.transpose(psum[:, turn_bank(UNITS * s + UNITS - 1), 0:P],
                                 recip_wide[:, s % 2].rearrange("p h d -> p (h d)"),
                                 ident[:]).then_inc(recip_turned, 1)

                def attend(s, part):
                    if part == 0:
                        if s >= 1:
                            pe.wait_ge(o_ready, at(b, SETS, s))
                        else:
                            pe.wait_ge(v_ready, at(b, VF, VF))
                        pe.wait_ge(even_taken, at(b, STEPS, HG * (s + 1)))
                        pe.wait_ge(odd_taken, at(b, STEPS, HG * (s + 1)))
                    tiles = range(NT)[part * NT // HG:(part + 1) * NT // HG]
                    for kt in tiles:
                        for hh in range(HG):
                            head = HG * (s // NT) + hh
                            ins = pe.matmul(psum[hh * HD:(hh + 1) * HD, O_BANK, 0:P],
                                            v[:, kt, head * HD:(head + 1) * HD], probsT_of(s)[:, hh, kt, :],
                                            start=(kt == 0), stop=(kt == NT - 1))
                    if part == HG - 1:
                        ins.then_inc(av_done, 1)

                def project(f):
                    pe.wait_ge(o_lo_ready, at(b, SETS, SETS - NT + 2 * f + 2))
                    rows_by_weight(f, f, WO).then_inc(proj_done, 1)

                for i in range(STEPS + T_LAG):
                    if i < STEPS:
                        score(i)
                    if i >= T_LAG:
                        turn(i - T_LAG)
                    if i >= R_LAG and (i - R_LAG) % HG == 0:
                        turn_recip((i - R_LAG) // HG)
                    if i >= AV_LAG:
                        attend((i - AV_LAG) // HG, (i - AV_LAG) % HG)
                for f in range(3):
                    project(f)
                for part in range(HG):
                    attend(SETS - 1, part)
                for f in range(3, VF):
                    project(f)


_INS = ["x", "adj", "L0_gnn_weight", "L0_gnn_bias", "L1_gnn_Wq", "L1_gnn_bq", "L1_gnn_Wk", "L1_gnn_bk",
        "L1_gnn_Wv", "L1_gnn_bv", "L1_gnn_Wo", "L1_gnn_bo"]


def kernel(**inputs):
    import numpy as np
    import concourse.bacc as bacc
    from concourse.bass_utils import run_bass_kernel_spmd

    nc = bacc.Bacc("TRN2", target_bir_lowering=False, num_devices=1)
    arrays, aps = {}, {}
    for name in _INS:
        a = np.ascontiguousarray(inputs[name])
        arrays[f"in_{name}"] = a
        aps[name] = nc.dram_tensor(f"in_{name}", a.shape, mybir.dt.from_np(a.dtype), kind="ExternalInput").ap()
    out = nc.dram_tensor("out", arrays["in_x"].shape, F32, kind="ExternalOutput").ap()
    weights = [aps[n] for n in ("L0_gnn_weight", "L1_gnn_Wq", "L1_gnn_Wk", "L1_gnn_Wv", "L1_gnn_Wo")]
    biases = [aps[n] for n in ("L0_gnn_bias", "L1_gnn_bq", "L1_gnn_bk", "L1_gnn_bv", "L1_gnn_bo")]
    build(nc, aps["x"], aps["adj"], weights, biases, out)
    result = run_bass_kernel_spmd(nc, [arrays], core_ids=[0])
    return result.results[0]["out"]
```

```python
from contextlib import ExitStack

import concourse.bass as bass
from concourse import mybir

F32 = mybir.dt.float32
F32R = mybir.dt.float32r
ALU = mybir.AluOpType
ACT = mybir.ActivationFunctionType

P = 128
BANK = 512
HEADS = 8
EPS = 1e-5
MASKED = 1.0e9
FAR = 3.0e38
WQ, WK, WV, WO = range(4)
MASK_PARTS = 4


def split_terms(hi_a, lo_a, hi_b, lo_b):
    return ((hi_a, hi_b), (lo_a, hi_b), (hi_a, lo_b))


def build(nc, x, adj, weights, biases, out):
    B, N, D = x.shape
    NT = N // P
    DC = D // P
    HALVES = N // BANK
    TPH = BANK // P
    HD = D // HEADS
    HG = P // HD
    GROUPS = HEADS // HG
    SCALE = float(HD) ** -0.5
    x1_dram = nc.dram_tensor("x1_rows", (B, N, D), F32, kind="Internal").ap()

    with ExitStack() as whole:
        def sb(ctx, name, shape, dt=F32):
            return ctx.enter_context(nc.sbuf_tensor(name, shape, dt))

        def sem(ctx, name):
            return ctx.enter_context(nc.semaphore(name))

        psum = whole.enter_context(nc.psum_tensor("psum", [P, 8, BANK], F32))
        ident = sb(whole, "ident", [P, P])
        mask = sb(whole, "mask", [P, NT, N])
        w_hi = sb(whole, "w_hi", [P, 4, DC, D], F32R)
        w_lo = sb(whole, "w_lo", [P, 4, DC, D], F32R)
        b_rows = sb(whole, "b_rows", [P, 2, D])
        b_cols = sb(whole, "b_cols", [P, 2, GROUPS])
        eps = sb(whole, "eps", [P, 1])
        x1 = sb(whole, "x1", [P, NT, D])
        h = sb(whole, "h", [P, NT, D])
        fT_hi = sb(whole, "fT_hi", [P, DC, N], F32R)
        fT_lo = sb(whole, "fT_lo", [P, DC, N], F32R)
        mask_ready = sem(whole, "mask_ready")
        x1_stored = sem(whole, "x1_stored")
        x1_loaded = sem(whole, "x1_loaded")

        shared = (psum, ident, mask, w_hi, w_lo, b_rows, b_cols, eps, x1, h, fT_hi, fT_lo,
                  mask_ready, x1_stored, x1_loaded)
        layer_norm_1(nc, sb, sem, x, adj, weights, biases, x1_dram, shared,
                     (B, N, D, NT, DC, HALVES, TPH, GROUPS, SCALE))
        layer_norm_2(nc, sb, sem, x1_dram, out, shared, (B, N, D, NT, DC, HALVES, TPH, HD, HG, GROUPS))


def layer_norm_1(nc, sb, sem, x, adj, weights, biases, x1_dram, shared, sizes):
    B, N, D, NT, DC, HALVES, TPH, GROUPS, SCALE = sizes
    (psum, ident, mask, w_hi, w_lo, b_rows, b_cols, eps, x1, h, fT_hi, fT_lo,
     mask_ready, x1_stored, x1_loaded) = shared
    CH = HALVES * DC
    HB = NT // 2
    PAIRS = B // 2
    XH = 2
    XT = NT // XH
    TURNS = HALVES * NT
    with ExitStack() as ctx:
        adjT_hi = sb(ctx, "adjT_hi", [P, NT, N], F32R)
        adjT_lo = sb(ctx, "adjT_lo", [P, NT, N], F32R)
        xin = sb(ctx, "xin", [P, 2, NT, D])
        x_hi = sb(ctx, "x_hi", [P, 2, NT, D], F32R)
        x_lo = sb(ctx, "x_lo", [P, 2, NT, D], F32R)
        w_in = x1[:].rearrange("p (i c) n -> p i c n", i=4)
        w0_in = sb(ctx, "w0_in", [P, DC, D])
        w0_hi = sb(ctx, "w0_hi", [P, DC, D], F32R)
        w0_lo = sb(ctx, "w0_lo", [P, DC, D], F32R)
        b_in = sb(ctx, "b_in", [P, 2, GROUPS])
        bias_row = sb(ctx, "bias_row", [P, 1, D])
        stats = sb(ctx, "stats", [P, NT, 6])
        moments = sb(ctx, "moments", [P, NT, 2])
        std = sb(ctx, "std", [P, NT])
        rstd = sb(ctx, "rstd", [P, NT])

        adj_loaded = [sem(ctx, f"adj_loaded{i}") for i in range(2 * HALVES)]
        w0_loaded = sem(ctx, "w0_loaded")
        w_loaded = sem(ctx, "w_loaded")
        bias_loaded = sem(ctx, "bias_loaded")
        b_loaded = sem(ctx, "b_loaded")
        x_loaded = [sem(ctx, f"x_loaded{u}") for u in range(2)]
        zeroed = sem(ctx, "zeroed")
        ident_ready = sem(ctx, "ident_ready")
        eps_ready = sem(ctx, "eps_ready")
        wq_scaled = sem(ctx, "wq_scaled")
        w0_hi_ready = sem(ctx, "w0_hi_ready")
        w0_lo_ready = sem(ctx, "w0_lo_ready")
        w_hi_ready = sem(ctx, "w_hi_ready")
        w_lo_ready = sem(ctx, "w_lo_ready")
        adj_turned = sem(ctx, "adj_turned")
        adjT_hi_ready = sem(ctx, "adjT_hi_ready")
        adjT_lo_ready = sem(ctx, "adjT_lo_ready")
        x_hi_ready = sem(ctx, "x_hi_ready")
        x_lo_ready = sem(ctx, "x_lo_ready")
        xb_ready = sem(ctx, "xb_ready")
        yT_done = sem(ctx, "yT_done")
        yT_hi_ready = sem(ctx, "yT_hi_ready")
        yT_lo_ready = sem(ctx, "yT_lo_ready")
        h_done = sem(ctx, "h_done")
        h_ready = sem(ctx, "h_ready")
        stats_ready = sem(ctx, "stats_ready")
        moments_ready = sem(ctx, "moments_ready")
        std_ready = sem(ctx, "std_ready")
        rstd_ready = sem(ctx, "rstd_ready")
        x1_ready = sem(ctx, "x1_ready")
        passed = sem(ctx, "passed")

        def rows(dram, b):
            return dram[b].rearrange("(t p) d -> p t d", p=P)

        def turn_bank(f):
            return f if f < NT else DC + (f - NT) % (8 - DC)

        block = ctx.enter_context(nc.Block())

        @block.sync
        def _(sp):
            adj_rows = adj.rearrange("(t p) m -> p t m", p=P)

            def load_adj(i):
                tiles, cols = slice(i // 2 * TPH, (i // 2 + 1) * TPH), slice(i % 2 * N // 2, (i % 2 + 1) * N // 2)
                sp.dma_start(mask[:, tiles, cols], adj_rows[:, tiles, cols]).then_inc(adj_loaded[i], 16)

            load_adj(0)
            sp.dma_start(xin[:, 0], rows(x, 0)).then_inc(x_loaded[0], 16)
            load_adj(1)
            sp.dma_start(w0_in[:], weights[0].rearrange("(c p) n -> p c n", p=P)).then_inc(w0_loaded, 16)
            load_adj(2)
            load_adj(3)
            sp.dma_start(bias_row[:, 0, :], biases[0].rearrange("(a d) -> a d", a=1).broadcast_to([P, D])) \
              .then_inc(bias_loaded, 16)
            sp.dma_start(xin[:, 1], rows(x, 1)).then_inc(x_loaded[1], 16)
            for i, w in enumerate(weights[1:]):
                sp.dma_start(w_in[:, i], w.rearrange("(c p) n -> p c n", p=P)).then_inc(w_loaded, 16)
            for i in range(2):
                sp.dma_start(b_rows[:, i, :], biases[3 + i].rearrange("(a d) -> a d", a=1).broadcast_to([P, D])) \
                  .then_inc(b_loaded, 16)
            with nc.allow_non_contiguous_dma(reason="one feature per partition"):
                for i in range(2):
                    sp.dma_start(b_in[:, i, :], biases[1 + i].rearrange("(g p) -> p g", p=P)) \
                      .then_inc(b_loaded, 16)
            with sp.Fori(0, PAIRS - 1) as j:
                for u in range(2):
                    sp.wait_ge(x1_ready, 2 * j + u + 1)
                    sp.dma_start(xin[:, u], rows(x, 2 * j + u + 2)).then_inc(x_loaded[u], 16)
                    sp.dma_start(rows(x1_dram, 2 * j + u), h[:]).then_inc(x1_stored, 16)
            sp.wait_ge(w_lo_ready, 1)
            sp.wait_ge(x1_stored, 16)
            sp.dma_start(x1[:], rows(x1_dram, 0)).then_inc(x1_loaded, 16)
            for b in (B - 2, B - 1):
                sp.wait_ge(x1_ready, b + 1)
                sp.dma_start(rows(x1_dram, b), h[:]).then_inc(x1_stored, 16)

        @block.gpsimd
        def _(pool):
            pool.memset(ident[:], 0.0).then_inc(zeroed, 1)
            pool.wait_ge(zeroed, 1)
            pool.affine_select(out=ident[:], in_=ident[:], compare_op=ALU.not_equal, fill=1.0, base=0,
                               pattern=[[-1, P]], channel_multiplier=1).then_inc(ident_ready, 1)
            pool.memset(eps[:], EPS).then_inc(eps_ready, 1)

            def x_low(b, u):
                for i in range(XH):
                    tiles = slice(i * XT, (i + 1) * XT)
                    pool.wait_ge(x_hi_ready, XH * b + i + 1)
                    pool.tensor_tensor(x_lo[:, u, tiles], xin[:, u, tiles], x_hi[:, u, tiles].bitcast(F32),
                                       ALU.subtract).then_inc(x_lo_ready, 1)

            def add_bias(b, u):
                pool.wait_ge(x_lo_ready, XH * b + XH)
                pool.tensor_tensor(xin[:, u], xin[:, u],
                                   bias_row[:].broadcast_to([P, NT, D]), ALU.add).then_inc(xb_ready, 1)

            x_low(0, 0)
            pool.wait_ge(w0_hi_ready, 1)
            pool.tensor_tensor(w0_lo[:], w0_in[:], w0_hi[:].bitcast(F32), ALU.subtract).then_inc(w0_lo_ready, 1)
            pool.wait_ge(bias_loaded, 16)
            add_bias(0, 0)
            x_low(1, 1)
            add_bias(1, 1)
            pool.wait_ge(w_hi_ready, 1)
            pool.tensor_tensor(w_lo[:], w_in[:], w_hi[:].bitcast(F32), ALU.subtract).then_inc(w_lo_ready, 1)
            with pool.Fori(1, PAIRS) as j:
                for u in range(2):
                    x_low(2 * j + u, u)
                    add_bias(2 * j + u, u)

        @block.scalar
        def _(act):
            def adj_high(f):
                act.wait_ge(adj_turned, f + 1)
                act.activation(adjT_hi[:, f % NT, (f // NT) * BANK:(f // NT + 1) * BANK], psum[:, turn_bank(f), :],
                               ACT.Copy).then_inc(adjT_hi_ready, 1)

            def x_high(u, loads):
                act.wait_ge(x_loaded[u], 16 * loads)
                for i in range(XH):
                    tiles = slice(i * XT, (i + 1) * XT)
                    act.activation(x_hi[:, u, tiles], xin[:, u, tiles], ACT.Copy).then_inc(x_hi_ready, 1)

            def y_high(b, c):
                hf, dc = divmod(c, DC)
                act.wait_ge(yT_done, CH * b + c + 1)
                act.activation(fT_hi[:, dc, hf * BANK:(hf + 1) * BANK], psum[:, c, :],
                               ACT.Copy).then_inc(yT_hi_ready, 1)

            def roots(b):
                act.wait_ge(moments_ready, b + 1)
                act.activation(std[:], moments[:, :, 1], ACT.Sqrt, bias=eps[:, 0:1]).then_inc(std_ready, 1)

            for f in range(NT // 2):
                adj_high(f)
            x_high(0, 1)
            for f in range(NT // 2, NT):
                adj_high(f)
            act.wait_ge(w0_loaded, 16)
            act.activation(w0_hi[:], w0_in[:], ACT.Copy).then_inc(w0_hi_ready, 1)
            y_high(0, 0)
            for f in range(NT, TURNS):
                adj_high(f)
            x_high(1, 1)
            y_high(0, 1)
            act.wait_ge(wq_scaled, 1)
            act.activation(w_hi[:], w_in[:], ACT.Copy).then_inc(w_hi_ready, 1)
            y_high(0, 2)
            y_high(0, 3)
            act.wait_ge(eps_ready, 1)

            def batch(b, u, loads, last):
                y_high(b, 0)
                roots(b - 1)
                y_high(b, 1)
                y_high(b, 2)
                if not last:
                    x_high(1 - u, loads)
                y_high(b, 3)

            with act.Fori(0, PAIRS - 1) as j:
                batch(2 * j + 1, 1, j + 2, False)
                batch(2 * j + 2, 0, j + 2, False)
            batch(B - 1, 1, None, True)
            roots(B - 1)

        @block.vector
        def _(dve):
            def adj_low(f):
                dve.wait_ge(adjT_hi_ready, f + 1)
                cols = slice((f // NT) * BANK, (f // NT + 1) * BANK)
                dve.tensor_tensor(adjT_lo[:, f % NT, cols], psum[:, turn_bank(f), :],
                                  adjT_hi[:, f % NT, cols].bitcast(F32), ALU.subtract).then_inc(adjT_lo_ready, 1)

            def y_low(b, c):
                hf, dc = divmod(c, DC)
                cols = slice(hf * BANK, (hf + 1) * BANK)
                dve.wait_ge(yT_hi_ready, CH * b + c + 1)
                dve.tensor_tensor(fT_lo[:, dc, cols], psum[:, c, :], fT_hi[:, dc, cols].bitcast(F32),
                                  ALU.subtract).then_inc(yT_lo_ready, 1)

            def residual(b, u, w):
                h2 = xin[:, u, 2 * w:2 * w + 2, :]
                dve.wait_ge(h_done, HB * b + w + 1)
                dve.tensor_tensor(h2, psum[:, CH + w, :].rearrange("p (t d) -> p t d", t=2), h2, ALU.add) \
                   .then_inc(h_ready, 1)

            def statistics(b, u, w):
                dve.wait_ge(h_ready, HB * b + w + 1)
                for t in (2 * w, 2 * w + 1):
                    dve.bn_stats(stats[:, t, :], xin[:, u, t, :]).then_inc(stats_ready, 1)

            def moments_of(b):
                dve.wait_ge(stats_ready, NT * b + NT)
                dve.sem_inc(passed, 1)
                for t in range(NT):
                    ins = dve.bn_aggr(moments[:, t, :], stats[:, t, :])
                ins.then_inc(moments_ready, 1)

            def normalise(b, u, stores):
                dve.wait_ge(std_ready, b + 1)
                dve.reciprocal(rstd[:], std[:]).then_inc(rstd_ready, 1)
                dve.wait_ge(rstd_ready, b + 1)
                if stores is not None:
                    dve.wait_ge(x1_stored, 16 * stores)
                for t in range(NT):
                    ins = dve.tensor_scalar(h[:, t, :], xin[:, u, t, :], moments[:, t, 0:1],
                                            rstd[:, t:t + 1], ALU.subtract, ALU.mult)
                ins.then_inc(x1_ready, 1)

            def first_half(b, u):
                dve.wait_ge(xb_ready, b + 1)
                for w in range(HB // 2):
                    residual(b, u, w)
                for w in range(HB // 2):
                    statistics(b, u, w)

            def second_half(b, u):
                for w in range(HB // 2, HB):
                    residual(b, u, w)
                for w in range(HB // 2, HB):
                    statistics(b, u, w)
                moments_of(b)

            def make_mask(i):
                part = mask[:, i * NT // MASK_PARTS:(i + 1) * NT // MASK_PARTS, :]
                dve.tensor_scalar(part, part, 1.0, -MASKED, ALU.subtract, ALU.mult).then_inc(mask_ready, 1)

            for f in range(NT):
                adj_low(f)
            y_low(0, 0)
            for f in range(NT, TURNS):
                adj_low(f)
            dve.wait_ge(w_loaded, 16 * 4)
            dve.tensor_scalar(w_in[:, WQ], w_in[:, WQ], -SCALE, None, ALU.mult).then_inc(wq_scaled, 1)
            y_low(0, 1)
            dve.wait_ge(adj_turned, TURNS)
            make_mask(0)
            dve.wait_ge(b_loaded, 16 * 4)
            dve.tensor_scalar(b_cols[:, 0, :], b_in[:, 0, :], -SCALE, None, ALU.mult)
            dve.tensor_copy(b_cols[:, 1, :], b_in[:, 1, :])
            y_low(0, 2)
            make_mask(1)
            first_half(0, 0)
            y_low(0, 3)
            make_mask(2)
            make_mask(3)

            def batch(b, u, stores):
                y_low(b, 0)
                second_half(b - 1, 1 - u)
                y_low(b, 1)
                normalise(b - 1, 1 - u, stores)
                y_low(b, 2)
                first_half(b, u)
                y_low(b, 3)

            batch(1, 1, None)
            with dve.Fori(1, PAIRS) as j:
                batch(2 * j, 0, 2 * j - 1)
                batch(2 * j + 1, 1, 2 * j)
            second_half(B - 1, 1)
            normalise(B - 1, 1, B - 1)

        @block.tensor
        def _(pe):
            def turn_adj(f):
                if f % NT in (0, NT // 2):
                    pe.wait_ge(adj_loaded[f // (NT // 2)], 16)
                if f >= NT:
                    pe.wait_ge(adjT_lo_ready, max(NT, f - (8 - DC) + 1))
                for t in range(TPH):
                    tile = f // NT * TPH + t
                    ins = pe.transpose(psum[:, turn_bank(f), t * P:(t + 1) * P],
                                       mask[:, tile, f % NT * P:(f % NT + 1) * P], ident[:])
                ins.then_inc(adj_turned, 1)

            def chunk(b, u, c, tiles=range(NT)):
                hf, dc = divmod(c, DC)
                for mt in tiles:
                    if c == 0 and mt % XT == 0:
                        pe.wait_ge(x_lo_ready, XH * b + mt // XT + 1)
                    cols = slice(hf * BANK, (hf + 1) * BANK)
                    terms = split_terms(x_hi[:, u, mt, dc * P:(dc + 1) * P], x_lo[:, u, mt, dc * P:(dc + 1) * P],
                                        adjT_hi[:, mt, cols], adjT_lo[:, mt, cols])
                    for n, (lhsT, rhs) in enumerate(terms):
                        ins = pe.matmul(psum[:, c, :], lhsT, rhs, start=(mt == 0 and n == 0),
                                        stop=(mt == NT - 1 and n == 2))
                if tiles[-1] == NT - 1:
                    ins.then_inc(yT_done, 1)

            def project(b, half):
                pe.wait_ge(yT_lo_ready, CH * b + DC * (half + 1))
                for w in range(half * HB // 2, (half + 1) * HB // 2):
                    for t in range(2):
                        cols = slice((2 * w + t) * P, (2 * w + t + 1) * P)
                        for dc in range(DC):
                            terms = split_terms(fT_hi[:, dc, cols], fT_lo[:, dc, cols], w0_hi[:, dc], w0_lo[:, dc])
                            for n, (lhsT, rhs) in enumerate(terms):
                                ins = pe.matmul(psum[:, CH + w, t * D:(t + 1) * D], lhsT, rhs,
                                                start=(dc == 0 and n == 0), stop=(dc == DC - 1 and n == 2))
                    ins.then_inc(h_done, 1)

            pe.wait_ge(ident_ready, 1)
            for f in range(NT):
                turn_adj(f)
            for mt in range(NT):
                pe.wait_ge(adjT_lo_ready, mt + 1)
                chunk(0, 0, 0, range(mt, mt + 1))
            for f in range(NT, TURNS):
                turn_adj(f)
            chunk(0, 0, 1)
            pe.wait_ge(adjT_lo_ready, TURNS)
            chunk(0, 0, 2)
            pe.wait_ge(w0_lo_ready, 1)
            project(0, 0)
            chunk(0, 0, 3)

            def batch(b, u):
                chunk(b, u, 0)
                project(b - 1, 1)
                chunk(b, u, 1)
                chunk(b, u, 2)
                project(b, 0)
                chunk(b, u, 3)

            batch(1, 1)
            with pe.Fori(1, PAIRS) as j:
                batch(2 * j, 0)
                batch(2 * j + 1, 1)
            project(B - 1, 1)


def layer_norm_2(nc, sb, sem, x1_dram, out, shared, sizes):
    B, N, D, NT, DC, HALVES, TPH, HD, HG, GROUPS = sizes
    (psum, ident, mask, w_hi, w_lo, b_rows, b_cols, eps, x1, h, fT_hi, fT_lo,
     mask_ready, x1_stored, x1_loaded) = shared
    XF = DC * HALVES
    QF = GROUPS * 2 * HALVES
    VF = NT // 2
    STEPS = HEADS * NT
    SETS = GROUPS * NT
    PARTS = 3
    T_LAG = 2
    R_LAG = HG - 1 + T_LAG
    AV_LAG = R_LAG + 1
    O_LAG = AV_LAG + HG
    W_LAG = O_LAG + 1
    S_LAG = W_LAG + 3
    POOL_SHARE = 3
    RING_BANK, RING = 4, 3
    O_BANK = 7
    with ExitStack() as ctx:
        q_parts = sb(ctx, "q_parts", [P, HEADS, N], F32R)
        k_parts = sb(ctx, "k_parts", [P, HEADS, N], F32R)
        v = sb(ctx, "v", [P, NT, D])
        probs = sb(ctx, "probs", [P, 2, N])
        probsT = sb(ctx, "probsT", [P, 2, HG * N])
        q1_staged = sb(ctx, "q1_staged", [P, 2, N])
        far = sb(ctx, "far", [P, STEPS])
        sums = sb(ctx, "sums", [P, SETS, HG])
        recip = sb(ctx, "recip", [P, SETS, HG])
        ones = sb(ctx, "ones", [P, HD])
        recip_wide = sb(ctx, "recip_wide", [P, HG, HD])
        warm = sb(ctx, "warm", [P, 1])
        recipT = sb(ctx, "recipT", [P, 2, P])
        o_full = sb(ctx, "o_full", [P, P])
        o_last_hi = sb(ctx, "o_last_hi", [P, GROUPS, P], F32R)
        o_last_lo = sb(ctx, "o_last_lo", [P, GROUPS, P], F32R)
        stats = sb(ctx, "stats2", [P, NT, 6])
        moments = sb(ctx, "moments2", [P, NT, 2])
        std = sb(ctx, "std2", [P, NT])
        rstd = sb(ctx, "rstd2", [P, NT])
        shift = sb(ctx, "shift", [P, NT])

        res_loaded = sem(ctx, "res_loaded")
        stored = sem(ctx, "stored")
        ones_ready = sem(ctx, "ones_ready")
        res_ready = sem(ctx, "res_ready")
        x1_turned = sem(ctx, "x1_turned")
        x1T_hi_ready = sem(ctx, "x1T_hi_ready")
        x1T_lo_ready = sem(ctx, "x1T_lo_ready")
        qk_done = sem(ctx, "qk_done")
        qk_hi_ready = sem(ctx, "qk_hi_ready")
        qk_lo_ready = sem(ctx, "qk_lo_ready")
        parts_placed = [sem(ctx, f"parts_placed{i}") for i in range(HEADS)]
        placed_by_pool = [sem(ctx, f"placed_by_pool{i}") for i in range(HEADS)]
        v_done = sem(ctx, "v_done")
        v_ready = sem(ctx, "v_ready")
        scores_done = sem(ctx, "scores_done")
        masked = sem(ctx, "masked")
        probs_ready = sem(ctx, "probs_ready")
        turned = sem(ctx, "turned")
        even_taken = sem(ctx, "even_taken")
        odd_taken = sem(ctx, "odd_taken")
        recip_ready = sem(ctx, "recip_ready")
        wide_ready = sem(ctx, "wide_ready")
        recip_turned = sem(ctx, "recip_turned")
        recipT_ready = sem(ctx, "recipT_ready")
        av_done = sem(ctx, "av_done")
        o_ready = sem(ctx, "o_ready")
        o_lo_ready = sem(ctx, "o_lo_ready")
        proj_done = sem(ctx, "proj_done")
        h_ready = sem(ctx, "h_ready2")
        stats_ready = sem(ctx, "stats_ready2")
        moments_ready = sem(ctx, "moments_ready2")
        std_ready = sem(ctx, "std_ready2")
        rstd_ready = sem(ctx, "rstd_ready2")
        shift_ready = sem(ctx, "shift_ready")
        normed = sem(ctx, "normed")
        normed_by_dve = sem(ctx, "normed_by_dve")
        passed = sem(ctx, "passed2")

        def rows(dram, b):
            return dram[b].rearrange("(t p) d -> p t d", p=P)

        def staged(g, which):
            if g == 0:
                return probsT[:, 1, 2 * which * N:2 * (which + 1) * N].rearrange("p (w n) -> p w n", w=2)
            return x1[:].rearrange("p (w t) d -> p w (t d)", w=2) if which else q1_staged[:]

        def probsT_of(g):
            return probsT[:, g % 2, :].rearrange("p (h k q) -> p h k q", h=HG, k=NT)

        def slot(i):
            return psum[:, 2 * (i % 2):2 * (i % 2) + 2, :].rearrange("p a n -> p (a n)")

        ring = []
        for i in range(STEPS + T_LAG):
            if i >= T_LAG:
                ring += [("even", i - T_LAG), ("odd", i - T_LAG)]
            if i >= R_LAG and (i - R_LAG) % HG == 0:
                ring.append(("recip", (i - R_LAG) // HG))
            if i >= W_LAG + HG * (SETS - NT) and (i - W_LAG) % HG == 0:
                ring.append(("proj", (i - W_LAG) // HG - (SETS - NT)))
        ring += [("proj", NT - 2), ("proj", NT - 1)]

        def ring_bank(kind, n):
            return RING_BANK + ring.index((kind, n)) % RING

        qk_banks = [ring_bank("recip", SETS - 1), O_BANK, ring_bank("proj", NT - 2), ring_bank("proj", NT - 1),
                    RING_BANK, RING_BANK + 1, O_BANK, RING_BANK + 2]

        def taken_before(bank, f):
            return max(n for n in range(f) if qk_banks[n] == bank) + 1

        def outputT(g, t):
            if t == NT - 1:
                return o_last_hi[:, g], o_last_lo[:, g]
            return fT_hi[:, g, t * P:(t + 1) * P], fT_lo[:, g, t * P:(t + 1) * P]

        def qk_unit(f):
            return f // 4, f // 2 % 2, f % 2

        late = {0: (QF - 2,), 1: (QF - 1,)}
        late_low = {0: (QF - 3,), 1: (QF - 2, QF - 1)}

        pool_copies = [(1, 0), (2, 0), (3, 0)]

        def wait_placed(engine, head, batches):
            by_pool = sum(PARTS for hd, which in pool_copies if hd == head)
            for semaphore, copies in ((parts_placed[head], 2 * PARTS - by_pool), (placed_by_pool[head], by_pool)):
                if copies:
                    engine.wait_ge(semaphore, 16 * copies * batches)

        def place_head(queue, g, hh, which):
            parts, order = ((q_parts, (0, 1, 0)), (k_parts, (0, 0, 1)))[which]
            for r, part in enumerate(order):
                queue.dma_start(parts[r * HD:(r + 1) * HD, HG * g + hh, :].bitcast(F32),
                                staged(g, which)[hh * HD:(hh + 1) * HD, part, :]) \
                     .then_inc((placed_by_pool if g == 0 and (hh, which) in pool_copies else parts_placed)
                               [HG * g + hh], 16)

        def at(b, per, n):
            assert n > 0
            return b * per + n

        block = ctx.enter_context(nc.Block())

        @block.sync
        def _(sp):
            def place(b, g):
                for hh in range(HG):
                    for which in range(2):
                        if hh == 0:
                            sp.wait_ge(qk_lo_ready, at(b, QF, 4 * g + 3 + which))
                        if g or (hh, which) not in pool_copies:
                            place_head(sp, g, hh, which)

            def load_x1(b):
                for head in range(HG, HEADS):
                    wait_placed(sp, head, b)
                sp.dma_start(x1[:], rows(x1_dram, b)).then_inc(x1_loaded, 16)

            def residual(b):
                sp.dma_start(h[:], rows(x1_dram, b)).then_inc(res_loaded, 16)

            def result(b):
                sp.wait_ge(normed, b + 1)
                sp.dma_start(rows(out, b), h[:]).then_inc(stored, 16)

            def batch(b, last):
                place(b + 1, 0)
                result(b)
                place(b + 1, 1)
                sp.wait_ge(stored, 16 * b + 16)
                residual(b + 1)
                if not last:
                    load_x1(b + 2)

            sp.wait_ge(x1_stored, 16 * B)
            residual(0)
            place(0, 0)
            place(0, 1)
            load_x1(1)
            with sp.Fori(0, B - 2) as b:
                batch(b, False)
            batch(B - 2, True)
            sp.wait_ge(normed, B)
            sp.dma_start(rows(out, B - 1)[:, 0:POOL_SHARE], h[:, 0:POOL_SHARE]).then_inc(stored, 16)
            sp.wait_ge(normed_by_dve, 1)
            sp.dma_start(rows(out, B - 1)[:, POOL_SHARE:NT], h[:, POOL_SHARE:NT]).then_inc(stored, 16)
            sp.wait_ge(stored, 16 * (B + 1))

        @block.gpsimd
        def _(pool):
            pool.memset(ones[:], 1.0).then_inc(ones_ready, 1)
            pool.wait_ge(ones_ready, 1)

            def place(b):
                for which in range(2):
                    pool.wait_ge(qk_lo_ready, at(b, QF, 3 + which))
                    pool.sem_inc(passed, 1)
                    for hh in range(HG):
                        if (hh, which) in pool_copies:
                            place_head(pool, 0, hh, which)

            def batch(b, last):
                def widen(s):
                    pool.wait_ge(recip_ready, at(b, SETS, s + 1))
                    if s >= 1:
                        pool.wait_ge(recip_turned, at(b, SETS, s))
                    pool.tensor_tensor(recip_wide[:], recip[:, s, :].rearrange("p (h a) -> p h a", a=1)
                                       .broadcast_to([P, HG, HD]),
                                       ones[:].rearrange("p (a d) -> p a d", a=1).broadcast_to([P, HG, HD]),
                                       ALU.mult).then_inc(wide_ready, 1)

                def o_low(s):
                    high, low = outputT(s // NT, s % NT)
                    pool.wait_ge(o_ready, at(b, SETS, s + 1))
                    pool.tensor_tensor(low, o_full[:], high.bitcast(F32), ALU.subtract) \
                        .then_inc(o_lo_ready, 1)

                for s in range(SETS + 1):
                    if s < SETS:
                        widen(s)
                    if s >= 1:
                        o_low(s - 1)
                    if s == 2:
                        pool.wait_ge(res_loaded, 16 * b + 16)
                        pool.tensor_tensor(h[:], h[:], b_rows[:, 1:2, :].broadcast_to([P, NT, D]), ALU.add) \
                            .then_inc(res_ready, 1)
                if not last:
                    place(b + 1)
                pool.wait_ge(shift_ready, b + 1)
                pool.sem_inc(passed, 1)
                for t in range(POOL_SHARE if last else NT):
                    ins = pool.tensor_scalar(h[:, t, :], h[:, t, :], rstd[:, t:t + 1], shift[:, t:t + 1],
                                             ALU.mult, ALU.add)
                ins.then_inc(normed, 1)

            place(0)
            with pool.Fori(0, B - 1) as b:
                batch(b, False)
            batch(B - 1, True)

        @block.scalar
        def _(act):
            def x1_high(b, f):
                half, dc = divmod(f, DC)
                act.wait_ge(x1_turned, at(b, XF, f + 1))
                act.activation(fT_hi[:, dc, half * BANK:(half + 1) * BANK], psum[:, f, :],
                               ACT.Copy).then_inc(x1T_hi_ready, 1)

            def qk_high(b, f):
                g, half, which = qk_unit(f)
                act.wait_ge(qk_done, at(b, QF, f + 1))
                act.activation(staged(g, which)[:, 0, half * BANK:(half + 1) * BANK].bitcast(F32R),
                               psum[:, qk_banks[f], :], ACT.Identity, bias=b_cols[:, which, g:g + 1]) \
                   .then_inc(qk_hi_ready, 1)

            def front(b, after=None):
                if after is None:
                    x1_high(b, 0)
                    x1_high(b, 1)
                x1_high(b, 2)
                x1_high(b, 3)
                for f in range(4):
                    qk_high(b, f)
                if after is not None:
                    roots(after)
                for f in range(4, QF - 2):
                    qk_high(b, f)

            def roots(b):
                act.wait_ge(moments_ready, b + 1)
                act.activation(std[:], moments[:, :, 1], ACT.Sqrt, bias=eps[:, 0:1]).then_inc(std_ready, 1)
                act.activation(warm[:], ones[:, 0:1], ACT.Exp)

            def attention(b, last):
                def take_even(i):
                    s, hh = divmod(i, HG)
                    if hh == 0:
                        if s >= 2:
                            act.wait_ge(av_done, at(b, SETS, s - 1))
                        if s == 1:
                            for head in range(HG):
                                wait_placed(act, head, b + 1)
                    act.wait_ge(turned, at(b, 2 * STEPS, 2 * i + 1))
                    act.activation(probsT_of(s)[:, hh, 0:TPH, :].rearrange("p k q -> p (k q)"),
                                   psum[:, ring_bank("even", i), :], ACT.Copy).then_inc(even_taken, 1)

                def exponentiate(i):
                    act.wait_ge(masked, at(b, STEPS, i + 1))
                    if i >= 2:
                        act.wait_ge(turned, at(b, 2 * STEPS, 2 * (i - 1)))
                    act.activation(probs[:, i % 2], slot(i), ACT.Exp, bias=far[:, i:i + 1], scale=-1.0,
                                   accum_out=sums[:, i // HG, i % HG:i % HG + 1]).then_inc(probs_ready, 1)

                def take_recip(s):
                    act.wait_ge(recip_turned, at(b, SETS, s + 1))
                    if s >= 2:
                        act.wait_ge(o_ready, at(b, SETS, s - 1))
                    act.activation(recipT[:, s % 2], psum[:, ring_bank("recip", s), 0:P], ACT.Copy) \
                       .then_inc(recipT_ready, 1)

                for i in range(STEPS + T_LAG):
                    if i >= T_LAG:
                        take_even(i - T_LAG)
                    for f in late.get(i, ()):
                        qk_high(b, f)
                    if i < STEPS:
                        exponentiate(i)
                    if i >= R_LAG and (i - R_LAG) % HG == 0:
                        take_recip((i - R_LAG) // HG)
                    if i >= STEPS and not last:
                        x1_high(b + 1, i - STEPS)

            front(0)
            with act.Fori(0, B - 1) as b:
                attention(b, False)
                front(b + 1, b)
            attention(B - 1, True)
            roots(B - 1)

        @block.vector
        def _(dve):
            def x1_low(b, f):
                half, dc = divmod(f, DC)
                cols = slice(half * BANK, (half + 1) * BANK)
                dve.wait_ge(x1T_hi_ready, at(b, XF, f + 1))
                dve.tensor_tensor(fT_lo[:, dc, cols], psum[:, f, :], fT_hi[:, dc, cols].bitcast(F32),
                                  ALU.subtract).then_inc(x1T_lo_ready, 1)

            def qk_low(b, f):
                g, half, which = qk_unit(f)
                cols = slice(half * BANK, (half + 1) * BANK)
                dve.wait_ge(qk_hi_ready, at(b, QF, f + 1))
                dve.scalar_tensor_tensor(out=staged(g, which)[:, 1, cols].bitcast(F32R),
                                         in0=psum[:, qk_banks[f], :], scalar=b_cols[:, which, g:g + 1],
                                         in1=staged(g, which)[:, 0, cols], op0=ALU.add, op1=ALU.subtract) \
                   .then_inc(qk_lo_ready, 1)

            def values(b, f):
                dve.wait_ge(v_done, at(b, VF, f + 1))
                dve.tensor_tensor(v[:, 2 * f:2 * f + 2, :], psum[:, f, :].rearrange("p (t d) -> p t d", t=2),
                                  b_rows[:, 0:1, :].broadcast_to([P, 2, D]), ALU.add).then_inc(v_ready, 1)

            def statistics(b, t):
                dve.wait_ge(h_ready, at(b, NT, t + 1))
                dve.bn_stats(stats[:, t, :], h[:, t, :]).then_inc(stats_ready, 1)

            def scale_and_shift(b):
                dve.wait_ge(std_ready, b + 1)
                dve.reciprocal(rstd[:], std[:]).then_inc(rstd_ready, 1)
                dve.wait_ge(rstd_ready, b + 1)
                dve.scalar_tensor_tensor(out=shift[:], in0=moments[:, :, 0], scalar=-1.0, in1=rstd[:],
                                         op0=ALU.mult, op1=ALU.mult).then_inc(shift_ready, 1)

            def aggregate(b):
                dve.wait_ge(stats_ready, at(b, NT, NT))
                dve.sem_inc(passed, 1)
                for t in range(NT):
                    ins = dve.bn_aggr(moments[:, t, :], stats[:, t, :])
                ins.then_inc(moments_ready, 1)

            def attention(b, last):
                def add_mask(i):
                    dve.wait_ge(mask_ready, MASK_PARTS)
                    dve.wait_ge(scores_done, at(b, STEPS, i + 1))
                    dve.sem_inc(passed, 1)
                    dve.tensor_tensor_reduce(slot(i), slot(i), mask[:, i // HG % NT, :], 1.0, FAR, ALU.add, ALU.min,
                                             far[:, i:i + 1]).then_inc(masked, 1)

                def take_odd(i):
                    s, hh = divmod(i, HG)
                    if hh == 0:
                        if s >= 2:
                            dve.wait_ge(av_done, at(b, SETS, s - 1))
                        if s == 1:
                            for head in range(HG):
                                wait_placed(dve, head, b + 1)
                    dve.wait_ge(turned, at(b, 2 * STEPS, 2 * i + 2))
                    dve.tensor_copy(probsT_of(s)[:, hh, TPH:NT, :].rearrange("p k q -> p (k q)"),
                                    psum[:, ring_bank("odd", i), :]).then_inc(odd_taken, 1)

                def reciprocals(s):
                    dve.wait_ge(probs_ready, at(b, STEPS, HG * (s + 1)))
                    dve.reciprocal(recip[:, s, :], sums[:, s, :]).then_inc(recip_ready, 1)

                def output(s):
                    dve.wait_ge(recipT_ready, at(b, SETS, s + 1))
                    if s >= 1:
                        dve.wait_ge(o_lo_ready, at(b, SETS, s))
                    dve.wait_ge(av_done, at(b, SETS, s + 1))
                    dve.tensor_tensor(o_full[:], psum[:, O_BANK, 0:P], recipT[:, s % 2], ALU.mult)
                    dve.tensor_tensor(outputT(s // NT, s % NT)[0], psum[:, O_BANK, 0:P], recipT[:, s % 2], ALU.mult) \
                       .then_inc(o_ready, 1)

                def residual(t):
                    if t == 0:
                        dve.wait_ge(res_ready, b + 1)
                    dve.wait_ge(proj_done, at(b, NT, t + 1))
                    dve.tensor_tensor(h[:, t, :], psum[:, ring_bank("proj", t), 0:D], h[:, t, :], ALU.add) \
                       .then_inc(h_ready, 1)

                for i in range(STEPS + T_LAG):
                    if i >= O_LAG and (i - O_LAG) % HG == 0:
                        output((i - O_LAG) // HG)
                    if i < STEPS:
                        add_mask(i)
                    for f in late_low.get(i, ()):
                        qk_low(b, f)
                    if i > W_LAG + HG * (SETS - NT) and (i - W_LAG - 1) % HG == 0:
                        residual((i - W_LAG - 1) // HG - (SETS - NT))
                    if i % HG == 0 and i >= HG:
                        reciprocals(i // HG - 1)
                    if i >= T_LAG:
                        take_odd(i - T_LAG)
                    if i >= S_LAG + HG * (SETS - NT) and (i - S_LAG) % HG == 0:
                        statistics(b, (i - S_LAG) // HG - (SETS - NT))
                output(SETS - 2)
                if not last:
                    x1_low(b + 1, 0)
                    x1_low(b + 1, 1)
                residual(NT - 2)
                output(SETS - 1)
                if not last:
                    x1_low(b + 1, 2)
                    x1_low(b + 1, 3)
                    qk_low(b + 1, 0)
                    qk_low(b + 1, 1)
                residual(NT - 1)
                for t in range((STEPS + T_LAG - 1 - S_LAG) // HG - (SETS - NT) + 1, NT):
                    statistics(b, t)
                if not last:
                    qk_low(b + 1, 2)
                aggregate(b)
                if not last:
                    qk_low(b + 1, 3)
                    values(b + 1, 0)
                    values(b + 1, 1)
                scale_and_shift(b)
                if not last:
                    values(b + 1, 2)
                    values(b + 1, 3)
                    qk_low(b + 1, 4)

            for f in range(XF):
                x1_low(0, f)
            for f in range(4):
                qk_low(0, f)
            for f in range(VF):
                values(0, f)
            qk_low(0, 4)
            with dve.Fori(0, B - 1) as b:
                attention(b, False)
            attention(B - 1, True)
            dve.wait_ge(shift_ready, B)
            for t in range(POOL_SHARE, NT):
                ins = dve.tensor_scalar(h[:, t, :], h[:, t, :], rstd[:, t:t + 1], shift[:, t:t + 1],
                                        ALU.mult, ALU.add)
            ins.then_inc(normed_by_dve, 1)

        @block.tensor
        def _(pe):
            def turn_x1(b, f):
                half, dc = divmod(f, DC)
                if f == 0:
                    pe.wait_ge(x1_loaded, 16 * b + 16)
                for t in range(TPH):
                    ins = pe.transpose(psum[:, f, t * P:(t + 1) * P], x1[:, half * TPH + t, dc * P:(dc + 1) * P],
                                       ident[:])
                ins.then_inc(x1_turned, 1)

            def project_qk(b, f, after=None):
                g, half, which = qk_unit(f)
                if f in (0, 2):
                    pe.wait_ge(x1T_lo_ready, at(b, XF, DC * (half + 1)))
                if f >= 4:
                    pe.wait_ge(qk_lo_ready, at(b, QF, taken_before(qk_banks[f], f)))
                elif after is not None:
                    if f == 0:
                        pe.wait_ge(recipT_ready, at(after, SETS, SETS))
                    elif f == 1:
                        pe.wait_ge(o_ready, at(after, SETS, SETS))
                    else:
                        pe.wait_ge(h_ready, at(after, NT, NT - 3 + f))
                outs, cols = slice(g * P, (g + 1) * P), slice(half * BANK, (half + 1) * BANK)
                for dc in range(DC):
                    terms = split_terms(w_hi[:, WQ + which, dc, outs], w_lo[:, WQ + which, dc, outs],
                                        fT_hi[:, dc, cols], fT_lo[:, dc, cols])
                    for n, (lhsT, rhs) in enumerate(terms):
                        ins = pe.matmul(psum[:, qk_banks[f], :], lhsT, rhs, start=(dc == 0 and n == 0),
                                        stop=(dc == DC - 1 and n == 2))
                ins.then_inc(qk_done, 1)

            def rows_by_weight(bank, slot_cols, tile, w, chunks=range(DC)):
                for dc in chunks:
                    terms = split_terms(*tile(dc), w_hi[:, w, dc], w_lo[:, w, dc])
                    for n, (lhsT, rhs) in enumerate(terms):
                        ins = pe.matmul(psum[:, bank, slot_cols], lhsT, rhs, start=(dc == 0 and n == 0),
                                        stop=(dc == DC - 1 and n == 2))
                return ins

            def project_v(b, f):
                pe.wait_ge(x1T_lo_ready, at(b, XF, DC * (f // 2 + 1)))
                for t in range(2):
                    cols = slice((2 * f + t) * P, (2 * f + t + 1) * P)
                    ins = rows_by_weight(f, slice(t * D, (t + 1) * D),
                                         lambda dc: (fT_hi[:, dc, cols], fT_lo[:, dc, cols]), WV)
                ins.then_inc(v_done, 1)

            def rest_of_front(b, after=None):
                for f in (2, 3):
                    project_qk(b, f, after)
                for f in range(VF):
                    project_v(b, f)
                for f in range(4, QF - 2):
                    project_qk(b, f)

            def attention(b, last):
                def score(i):
                    s, hh = divmod(i, HG)
                    head, qt = HG * (s // NT) + hh, s % NT
                    if i % (HG * NT) < HG:
                        wait_placed(pe, head, b + 1)
                    if i < 2:
                        pe.wait_ge(v_ready, at(b, VF, 2 * i + 2))
                    else:
                        pe.wait_ge(probs_ready, at(b, STEPS, i - 1))
                    for half in range(HALVES):
                        ins = pe.matmul(psum[:, 2 * (i % 2) + half, :], q_parts[0:PARTS * HD, head, qt * P:(qt + 1) * P],
                                        k_parts[0:PARTS * HD, head, half * BANK:(half + 1) * BANK], start=True, stop=True)
                    ins.then_inc(scores_done, 1)

                def wait_ring(kind, n):
                    position = ring.index((kind, n))
                    if position < RING:
                        pe.wait_ge(qk_lo_ready, at(b, QF, taken_before(RING_BANK + position, QF)))
                        return
                    kind, n = ring[position - RING]
                    if kind == "even":
                        pe.wait_ge(even_taken, at(b, STEPS, n + 1))
                    elif kind == "odd":
                        pe.wait_ge(odd_taken, at(b, STEPS, n + 1))
                    elif kind == "recip":
                        pe.wait_ge(recipT_ready, at(b, SETS, n + 1))
                    else:
                        pe.wait_ge(h_ready, at(b, NT, n + 1))

                def turn(i):
                    pe.wait_ge(probs_ready, at(b, STEPS, i + 1))
                    for half, kind in enumerate(("even", "odd")):
                        wait_ring(kind, i)
                        for t in range(TPH):
                            kt = half * TPH + t
                            ins = pe.transpose(psum[:, ring_bank(kind, i), t * P:(t + 1) * P],
                                               probs[:, i % 2, kt * P:(kt + 1) * P], ident[:])
                        ins.then_inc(turned, 1)

                def turn_recip(s):
                    pe.wait_ge(wide_ready, at(b, SETS, s + 1))
                    wait_ring("recip", s)
                    pe.transpose(psum[:, ring_bank("recip", s), 0:P],
                                 recip_wide[:].rearrange("p h d -> p (h d)"),
                                 ident[:]).then_inc(recip_turned, 1)

                def attend(s, part):
                    if part == 0:
                        if s >= 1:
                            pe.wait_ge(o_ready, at(b, SETS, s))
                        pe.wait_ge(even_taken, at(b, STEPS, HG * (s + 1)))
                        pe.wait_ge(odd_taken, at(b, STEPS, HG * (s + 1)))
                    tiles = range(NT)[part * NT // HG:(part + 1) * NT // HG]
                    for kt in tiles:
                        for hh in range(HG):
                            head = HG * (s // NT) + hh
                            ins = pe.matmul(psum[hh * HD:(hh + 1) * HD, O_BANK, 0:P],
                                            v[:, kt, head * HD:(head + 1) * HD], probsT_of(s)[:, hh, kt, :],
                                            start=(kt == 0), stop=(kt == NT - 1))
                    if part == HG - 1:
                        ins.then_inc(av_done, 1)

                def project(t, chunks=range(DC)):
                    if chunks[0] == 0:
                        wait_ring("proj", t)
                    if chunks[-1] == DC - 1:
                        pe.wait_ge(o_lo_ready, at(b, SETS, SETS - NT + t + 1))
                    ins = rows_by_weight(ring_bank("proj", t), slice(0, D), lambda g: outputT(g, t), WO, chunks)
                    if chunks[-1] == DC - 1:
                        ins.then_inc(proj_done, 1)

                for i in range(STEPS + T_LAG):
                    if i < STEPS:
                        score(i)
                    for f in late.get(i, ()):
                        project_qk(b, f)
                    if i > W_LAG + HG * (SETS - NT) and (i - W_LAG - 1) % HG == 0:
                        project((i - W_LAG - 1) // HG - (SETS - NT), range(DC // 2, DC))
                    if i >= T_LAG:
                        turn(i - T_LAG)
                    if i >= R_LAG and (i - R_LAG) % HG == 0:
                        turn_recip((i - R_LAG) // HG)
                    if i >= W_LAG + HG * (SETS - NT) and (i - W_LAG) % HG == 0:
                        project((i - W_LAG) // HG - (SETS - NT), range(0, DC // 2))
                    if i >= AV_LAG:
                        attend((i - AV_LAG) // HG, (i - AV_LAG) % HG)
                    if i >= STEPS and not last:
                        turn_x1(b + 1, i - STEPS)
                attend(SETS - 1, 0)
                attend(SETS - 1, 1)
                project(NT - 2)
                attend(SETS - 1, 2)
                attend(SETS - 1, 3)
                if not last:
                    turn_x1(b + 1, 2)
                    turn_x1(b + 1, 3)
                    project_qk(b + 1, 0, b)
                    project_qk(b + 1, 1, b)
                project(NT - 1)
                if not last:
                    rest_of_front(b + 1, b)

            for f in range(XF):
                turn_x1(0, f)
            for f in (0, 1):
                project_qk(0, f)
            rest_of_front(0)
            with pe.Fori(0, B - 1) as b:
                attention(b, False)
            attention(B - 1, True)


_INS = ["x", "adj", "L0_gnn_weight", "L0_gnn_bias", "L1_gnn_Wq", "L1_gnn_bq", "L1_gnn_Wk", "L1_gnn_bk",
        "L1_gnn_Wv", "L1_gnn_bv", "L1_gnn_Wo", "L1_gnn_bo"]


def kernel(**inputs):
    import numpy as np
    import concourse.bacc as bacc
    from concourse.bass_utils import run_bass_kernel_spmd

    nc = bacc.Bacc("TRN2", target_bir_lowering=False, num_devices=1)
    arrays, aps = {}, {}
    for name in _INS:
        a = np.ascontiguousarray(inputs[name])
        arrays[f"in_{name}"] = a
        aps[name] = nc.dram_tensor(f"in_{name}", a.shape, mybir.dt.from_np(a.dtype), kind="ExternalInput").ap()
    out = nc.dram_tensor("out", arrays["in_x"].shape, F32, kind="ExternalOutput").ap()
    weights = [aps[n] for n in ("L0_gnn_weight", "L1_gnn_Wq", "L1_gnn_Wk", "L1_gnn_Wv", "L1_gnn_Wo")]
    biases = [aps[n] for n in ("L0_gnn_bias", "L1_gnn_bq", "L1_gnn_bk", "L1_gnn_bv", "L1_gnn_bo")]
    build(nc, aps["x"], aps["adj"], weights, biases, out)
    result = run_bass_kernel_spmd(nc, [arrays], core_ids=[0])
    return result.results[0]["out"]
```
